# Optimizing a Trainium2 kernel written in Bass

```python
import numpy as np
import jax
import jax.numpy as jnp

def _softmax(x, axis=-1):
    return jax.nn.softmax(x, axis=axis)

def _gelu(x):
    return jax.nn.gelu(x, approximate=True)

def _silu(x):
    return jax.nn.silu(x)

def _sigmoid(x):
    return jax.nn.sigmoid(x)

def _layernorm(x, axis=-1, eps=1e-05):
    m = jnp.mean(x, axis=axis, keepdims=True)
    v = jnp.var(x, axis=axis, keepdims=True)
    return (x - m) / jnp.sqrt(v + eps)

def _scatter_add(tgt, idx, src, axis=0):
    return tgt.at[idx].add(src)

def _segment_sum(src, seg, n):
    return jax.ops.segment_sum(src, seg, n)
kernel_name = 'mk_adaln_d1_jaxref_r4_396dff'

def setup_inputs(seed: int=0):
    np.random.seed(seed)
    _w = jnp.asarray

    def _L0_attn_setup():
        import jax, jax.numpy as jnp
        import numpy as np
        D_MODEL = 256
        N_HEADS = 16
        D_K = D_MODEL // N_HEADS
        key = jax.random.key(seed)
        ks = jax.random.split(key, 9)
        B, L = (2, 512)
        s = 1.0 / np.sqrt(D_MODEL)
        return {'x': jax.random.normal(ks[0], (B, L, D_MODEL), dtype=jnp.float32), 'Wq': jax.random.normal(ks[1], (D_MODEL, D_MODEL), dtype=jnp.float32) * s, 'bq': jnp.zeros((D_MODEL,), dtype=jnp.float32), 'Wk': jax.random.normal(ks[2], (D_MODEL, D_MODEL), dtype=jnp.float32) * s, 'bk': jnp.zeros((D_MODEL,), dtype=jnp.float32), 'Wv': jax.random.normal(ks[3], (D_MODEL, D_MODEL), dtype=jnp.float32) * s, 'bv': jnp.zeros((D_MODEL,), dtype=jnp.float32), 'Wo': jax.random.normal(ks[4], (D_MODEL, D_MODEL), dtype=jnp.float32) * s, 'bo': jnp.zeros((D_MODEL,), dtype=jnp.float32)}
    _L0_attn_in = _L0_attn_setup()

    def _L0_ffn_setup():
        import jax, jax.numpy as jnp
        import numpy as np
        from jax import lax
        T, B, I, M, O = (64, 64, 256, 256, 256)

        def _xavier(key, shape):
            fan_out, fan_in = shape
            limit = float(np.sqrt(6.0 / (fan_in + fan_out)))
            return jax.random.uniform(key, shape, jnp.float32, -limit, limit)
        key = jax.random.key(seed)
        ks = jax.random.split(key, 9)
        x = jax.random.normal(ks[0], (T, B, I), jnp.float32)
        return {'x': x, 'wf': _xavier(ks[1], (M, I)), 'uf': _xavier(ks[2], (M, M)), 'bf': jnp.zeros((M,), jnp.float32), 'wi': _xavier(ks[3], (M, I)), 'ui': _xavier(ks[4], (M, M)), 'bi': jnp.zeros((M,), jnp.float32), 'wc': _xavier(ks[5], (M, I)), 'uc': _xavier(ks[6], (M, M)), 'bc': jnp.zeros((M,), jnp.float32), 'wo': _xavier(ks[7], (O, I)), 'uo': _xavier(ks[8], (O, M)), 'bo': jnp.zeros((O,), jnp.float32), 'in_c': jnp.zeros((M,), jnp.float32)}
    _L0_ffn_in = _L0_ffn_setup()
    _L0_c = _w((lambda *s: np.random.randn(*s).astype(np.float32) * 0.05)(4, 256))
    _L0_wmod = _w((lambda *s: np.random.randn(*s).astype(np.float32) * 0.05)(256, 6 * 256) * 256 ** (-0.5))
    _d = {'L0_attn_x': _L0_attn_in['x'], 'L0_attn_Wq': _L0_attn_in['Wq'], 'L0_attn_bq': _L0_attn_in['bq'], 'L0_attn_Wk': _L0_attn_in['Wk'], 'L0_attn_bk': _L0_attn_in['bk'], 'L0_attn_Wv': _L0_attn_in['Wv'], 'L0_attn_bv': _L0_attn_in['bv'], 'L0_attn_Wo': _L0_attn_in['Wo'], 'L0_attn_bo': _L0_attn_in['bo'], 'L0_ffn_wf': _L0_ffn_in['wf'], 'L0_ffn_uf': _L0_ffn_in['uf'], 'L0_ffn_bf': _L0_ffn_in['bf'], 'L0_ffn_wi': _L0_ffn_in['wi'], 'L0_ffn_ui': _L0_ffn_in['ui'], 'L0_ffn_bi': _L0_ffn_in['bi'], 'L0_ffn_wc': _L0_ffn_in['wc'], 'L0_ffn_uc': _L0_ffn_in['uc'], 'L0_ffn_bc': _L0_ffn_in['bc'], 'L0_ffn_wo': _L0_ffn_in['wo'], 'L0_ffn_uo': _L0_ffn_in['uo'], 'L0_ffn_bo': _L0_ffn_in['bo'], 'L0_ffn_in_c': _L0_ffn_in['in_c'], 'L0_c': _L0_c, 'L0_wmod': _L0_wmod}
    _x0 = _d['L0_attn_x']
    _d['L0_attn_x'] = jax.random.normal(jax.random.fold_in(jax.random.key(seed), 1), (4, 1024, 256), dtype=_x0.dtype)
    del _x0
    return _d

def reference(L0_attn_x, L0_attn_Wq, L0_attn_bq, L0_attn_Wk, L0_attn_bk, L0_attn_Wv, L0_attn_bv, L0_attn_Wo, L0_attn_bo, L0_ffn_wf, L0_ffn_uf, L0_ffn_bf, L0_ffn_wi, L0_ffn_ui, L0_ffn_bi, L0_ffn_wc, L0_ffn_uc, L0_ffn_bc, L0_ffn_wo, L0_ffn_uo, L0_ffn_bo, L0_ffn_in_c, L0_c, L0_wmod):

    def _L0_attn_ref(x, Wq, bq, Wk, bk, Wv, bv, Wo, bo):
        import jax, jax.numpy as jnp
        import numpy as np
        D_MODEL = 256
        N_HEADS = 16
        D_K = D_MODEL // N_HEADS
        B, L, D = x.shape
        H, dk = (N_HEADS, D_K)

        def proj(W, b):
            y = jnp.einsum('bld,ed->ble', x, W) + b
            return y.reshape(B, L, H, dk).transpose(0, 2, 1, 3)
        Q = proj(Wq, bq)
        K = proj(Wk, bk)
        V = proj(Wv, bv)
        scores = jnp.einsum('bhqd,bhkd->bhqk', Q, K) / jnp.sqrt(jnp.float32(dk))
        probs = jax.nn.softmax(scores, axis=-1)
        col_scale = jnp.where(jnp.arange(L) == 0, 0.5, 1.0).astype(probs.dtype)
        combined = probs * col_scale
        out = jnp.einsum('bhqk,bhkd->bhqd', combined, V)
        out = out.transpose(0, 2, 1, 3).reshape(B, L, D)
        return jnp.einsum('bld,ed->ble', out, Wo) + bo

    def _L0_ffn_ref(x, wf, uf, bf, wi, ui, bi, wc, uc, bc, wo, uo, bo, in_c):
        import jax, jax.numpy as jnp
        import numpy as np
        from jax import lax
        T, B, I, M, O = (64, 64, 256, 256, 256)

        def _xavier(key, shape):
            fan_out, fan_in = shape
            limit = float(np.sqrt(6.0 / (fan_in + fan_out)))
            return jax.random.uniform(key, shape, jnp.float32, -limit, limit)
        batch = x.shape[1]
        c0 = jnp.broadcast_to(in_c, (batch, in_c.shape[0]))

        def step(c, xt):
            ft = jax.nn.sigmoid(xt @ wf.T + c @ uf.T + bf)
            it = jax.nn.sigmoid(xt @ wi.T + c @ ui.T + bi)
            gt = jnp.tanh(xt @ wc.T + c @ uc.T + bc)
            c = ft * c + it * gt
            return (c, None)
        c_final, _ = lax.scan(step, c0, x)
        h = jnp.tanh(jnp.einsum('tbi,oi->tbo', x, wo) + c_final @ uo.T + bo)
        return h
    x = L0_attn_x
    mod = (_silu(L0_c) @ L0_wmod).reshape(L0_c.shape[0], 6, 1, -1)
    sa, ca, ga, sb, cb, gb = (mod[:, 0], mod[:, 1], mod[:, 2], mod[:, 3], mod[:, 4], mod[:, 5])
    ga = (2 * (ga >= 0) - 1) * jnp.maximum(jnp.abs(ga), 0.25)
    gb = (2 * (gb >= 0) - 1) * jnp.maximum(jnp.abs(gb), 0.25)
    h = _layernorm(x, axis=-1) * (1 + ca) + sa
    x = x + ga * _L0_attn_ref(h, L0_attn_Wq, L0_attn_bq, L0_attn_Wk, L0_attn_bk, L0_attn_Wv, L0_attn_bv, L0_attn_Wo, L0_attn_bo)
    h = _layernorm(x, axis=-1) * (1 + cb) + sb
    x = x + gb * _L0_ffn_ref(h, L0_ffn_wf, L0_ffn_uf, L0_ffn_bf, L0_ffn_wi, L0_ffn_ui, L0_ffn_bi, L0_ffn_wc, L0_ffn_uc, L0_ffn_bc, L0_ffn_wo, L0_ffn_uo, L0_ffn_bo, L0_ffn_in_c)
    return x

_drawn_inputs = setup_inputs


def setup_inputs(seed=0):
    import zlib

    import numpy as np

    out = dict(_drawn_inputs(seed))
    spreads = {'L0_attn_bq': (0.0, 0.8),
     'L0_attn_bk': (0.0, 2.0),
     'L0_attn_bv': (0.0, 0.329),
     'L0_attn_bo': (0.0, 0.329),
     'L0_ffn_bf': (0.0, 2.0),
     'L0_ffn_bi': (0.0, 2.0),
     'L0_ffn_bc': (0.0, 0.754),
     'L0_ffn_bo': (0.0, 0.476),
     'L0_ffn_in_c': (0.0, 0.8)}
    factors = {'L0_attn_Wq': 2.887,
     'L0_attn_Wk': 2.735,
     'L0_ffn_wf': 3.285,
     'L0_ffn_uf': 6.97,
     'L0_ffn_ui': 4.802}
    for name, (base, spread) in spreads.items():
        noise = np.random.default_rng([zlib.crc32(name.encode()), seed]).standard_normal(out[name].shape)
        drawn = base * np.exp(spread * noise) if base else spread * noise
        out[name] = jnp.asarray(drawn.astype(out[name].dtype))
    for name, factor in factors.items():
        out[name] = (out[name] * factor).astype(out[name].dtype)
    return out
```

```python
from contextlib import ExitStack

import concourse.bass as bass
from concourse import mybir

F32 = mybir.dt.float32
BF16 = mybir.dt.bfloat16
ALU = mybir.AluOpType
ACT = mybir.ActivationFunctionType
AX = mybir.AxisListType

P = 128
BATCH, L, D = 4, 1024, 256
HEADS = 16
DK = D // HEADS
DT = D // P
TT = L // P
HALF = L // 2
GROUPS = HEADS // 2
KT = L // P
STEPS = GROUPS * KT
RING = 4
STACK = 6 * DK
ROWS = STACK + 3
VW = DK + 1
VPITCH = HEADS * VW + 16
SCALE = DK ** -0.5
EPS = 1e-5
GATES = 3

WQ, WK, WV, WO, WF, WI, WC, WX, UF, UI, UC, UO = range(12)
BQ, BK, BF, BI, BC, C0 = range(6)
BV, BO, BH = range(3)
SA, CA, SB, CB = range(4)
MOD_COLS = (0, 1, 3, 4)
GA, GB = 2, 5

PRODUCTS = ((0, 0), (0, 1), (0, 2), (1, 0), (1, 1), (2, 0))
BLOCKS = [(n, qk, product[qk]) for n, product in enumerate(PRODUCTS) for qk in range(2)]

V_CHUNKS = ((0, 4), (5, 5), (6, 6), (7, 7))


def chunk_of(hp):
    return max(0, hp - 4)


class Phase:

    QKV = [("hT", 4), ("q", 4), ("k", 4), ("v", 4)]
    POST = [("oT", 4), ("wo", 4)]
    FFN = [("h2T", 4), ("gate", 12), ("pre", 4)]

    def __init__(self, b, base, qkv, post, plan=None):
        self.b, self.base, self.qkv, self.post = b, base, qkv, post
        self.plan = self.of_steps() if plan is None else plan
        self.order = {(name, k): n for n, (_, name, k) in enumerate(self.plan)}
        self.at = {step: (name, k) for step, name, k in self.plan}

    def of_steps(self):
        free = [i for i in range(STEPS) if i % KT not in (2, 3)]
        dense = [(n, k) for n, c in self.POST + self.QKV + self.FFN for k in range(c)]
        plan = []
        for i, (name, k) in zip(free[2:], dense):
            if self.qkv if (name, 4) in self.QKV else self.post:
                plan.append((i, name, k))
        for hp in range(GROUPS):
            if self.post or hp:
                plan.append((hp * KT + 2, "norm", hp))
            if self.qkv or hp < GROUPS - 1:
                plan.append((hp * KT + 3, "maxT", hp))
        return sorted(plan)

    def filled(self, name, k):
        return self.base + self.order[name, k] + 1


def planned(*parts):
    return [(None, name, k) for name, ks in parts for k in ks]


PROLOGUE = planned(("modT", [0]), ("mod_rows", range(4)), ("hT", range(4)), ("q", range(4)),
                   ("k", range(4)), ("v", range(4)), ("maxT", [GROUPS - 1]))
TAIL = planned(("norm", [0]), ("oT", range(4)), ("wo", range(4)), ("h2T", range(4)),
               ("gate", range(12)), ("pre", range(4)), ("fin", range(4)))


def phases():
    before = Phase(-1, 0, True, False, PROLOGUE)
    first = Phase(0, len(before.plan), True, False)
    start = first.base + len(first.plan)
    size = len(Phase(1, 0, True, True).plan)

    def mid(b):
        return Phase(b, start + (b - 1) * size, True, True)

    last = Phase(BATCH - 1, start + (BATCH - 2) * size, False, True)
    after = Phase(BATCH, last.base + len(last.plan), False, True, TAIL)
    return before, first, mid, last, after


def wait_past(eng, sem, value):
    if not isinstance(value, int) or value > 0:
        eng.wait_ge(sem, value)


def adaln_layer(nc, x, w_all, cols_in, rows_in, cT, wmod_in, pieces, x1_spill, pre_spill, out):
    ctx = ExitStack()
    with ctx:
        def sb(name, shape, dt=F32):
            return ctx.enter_context(nc.sbuf_tensor(name, shape, dt))[:]

        def pb(name, shape, dt=F32):
            return ctx.enter_context(nc.psum_tensor(name, shape, dt))[:]

        def sem(name):
            return ctx.enter_context(nc.semaphore(name))

        stack = sb("stack", [P, RING, 2, 2, L], BF16)
        probs = sb("probs", [P, 2, 2, L])
        v_now = sb("v_now", [P, KT, VPITCH])
        v_next = sb("v_next", [P, KT, VPITCH])
        w = sb("w", [P, 12, DT, D])
        cols = sb("cols", [P, 6, DT])
        rows = sb("rows", [P, 3, D])
        xn = sb("xn", [P, TT, D])
        x1 = sb("x1", [P, TT, D])
        o_tok = sb("o_tok", [P, TT, D])
        hT = sb("hT", [P, DT, L])
        fT = sb("fT", [P, DT, L])
        cell = sb("cell", [P, DT, L])
        cell_sum = sb("cell_sum", [P, DT, HALF])
        gates = sb("gates", [P, 2, GATES, HALF])
        qk_f32 = sb("qk_f32", [P, 2, HALF])
        rest = sb("rest", [P, HALF])
        parts = sb("parts", [P, 2, 3, HALF], BF16)
        attn = sb("attn", [P, 2, 2, D])
        pre = sb("pre", [P, 2, 2, D])
        o_raw = sb("o_raw", [P, HALF])
        inv_sum = sb("inv_sum", [P, 4, 4])
        max_half = sb("max_half", [P, 2, 2 * TT * 2])
        neg_max = sb("neg_max", [P, TT, 2])
        max_rest = sb("max_rest", [P, TT, 2])
        max_parts = sb("max_parts", [P, TT, 2, 3], BF16)
        max_rows = sb("max_rows", [6, L], BF16)
        cs = sb("cs", [P, DT, BATCH])
        cs_tanh = sb("cs_tanh", [P, DT, BATCH])
        silu = sb("silu", [P, DT, BATCH])
        silu_wide = sb("silu_wide", [P, DT, BATCH, P])
        modT = sb("modT", [P, 4, DT, BATCH])
        mod_rows = sb("mod_rows", [P, 2, BATCH, D])
        mod_sign = sb("mod_sign", [P, 2, BATCH, D])
        ga_bo = mod_sign[:, 0]
        stats = sb("stats", [P, 2, TT, 6])
        mean_var = sb("mean_var", [P, 2, TT, 2])
        var_eps = sb("var_eps", [P, 2, TT])
        rstd = sb("rstd", [P, 2, TT])
        minus_half = sb("minus_half", [P, TT])
        ident = sb("ident", [P, P])
        ident_bf = sb("ident_bf", [P, P], BF16)
        wmod = probs.rearrange("p a h l -> p (a h l)")[:, 0:DT * 6 * D].rearrange("p (t n) -> p t n", t=DT)
        pre_all = stack.rearrange("p s k h l -> p (s k h l)").bitcast(F32).rearrange(
            "p (t n d) -> p t n d", t=BATCH, d=D)
        x1_chunk = probs.rearrange("p a h l -> p a (h l)").rearrange("p a (t n d) -> p a t n d", t=BATCH, d=D)
        result = [xn.rearrange("p (t n) d -> p t n d", t=BATCH),
                  hT.rearrange("p a l -> p (a l)").rearrange("p (t n d) -> p t n d", t=BATCH, d=D)]

        scoresT = [pb(f"scoresT{h}", [P, 2, HALF]) for h in range(2)]
        scores = [pb(f"scores{i}", [P, HALF]) for i in range(2)]
        acc = pb("acc", [P, HALF])
        aux = pb("aux", [P, HALF])
        aux_bf = aux.bitcast(BF16)
        aux_tok = aux.rearrange("p (c e) -> p c e", c=2)

        mod_in = sem("mod_in")
        qkv_in = sem("qkv_in")
        rest_in = sem("rest_in")
        xn_in = sem("xn_in")
        res_in = sem("res_in")
        waited = sem("waited")
        zeros = sem("zeros")
        consts = sem("consts")
        filled_once = sem("filled_once")
        mod_seq = sem("mod_seq")
        cs_tanhed = sem("cs_tanhed")
        silu_ready = sem("silu_ready")
        mod_ready = sem("mod_ready")
        scoresT_full = sem("scoresT_full")
        exp_done = sem("exp_done")
        pv_done = sem("pv_done")
        acc_used = sem("acc_used")
        scores_full = sem("scores_full")
        scores_used = sem("scores_used")
        max_seq = sem("max_seq")
        max_split = sem("max_split")
        max_loaded = sem("max_loaded")
        aux_full = sem("aux_full")
        aux_used = sem("aux_used")
        sums_inverted = sem("sums_inverted")
        stack_in = [sem(f"stack_in{s}") for s in range(RING)]
        v_in = [sem(f"v_in{c}") for c in range(len(V_CHUNKS))]
        v_added = sem("v_added")
        ln_seq = [sem(f"ln_seq{n}") for n in range(2)]
        var_ready = [sem(f"var_ready{n}") for n in range(2)]
        rstd_ready = [sem(f"rstd_ready{n}") for n in range(2)]
        ln_done = [sem(f"ln_done{n}") for n in range(2)]
        split_seq = sem("split_seq")
        split_done = sem("split_done")
        parts_out = [sem(f"parts_out{n}") for n in range(2)]
        res_biased = sem("res_biased")
        attn_ready = sem("attn_ready")
        x1_ready = sem("x1_ready")
        x1_out = sem("x1_out")
        pre_ready = sem("pre_ready")
        pre_out = [sem(f"pre_out{n}") for n in range(2)]
        gate_seq = sem("gate_seq")
        gate_sum = sem("gate_sum")
        cell_ready = sem("cell_ready")
        pre_in = sem("pre_in")
        x1_in = [sem(f"x1_in{n}") for n in range(2)]
        last_sum = sem("last_sum")
        last_tanh = sem("last_tanh")
        last_gated = sem("last_gated")
        result_ready = sem("result_ready")
        out_done = [sem(f"out_done{n}") for n in range(2)]

        def alone(eng):
            eng.sem_inc(waited, 1)

        block = ctx.enter_context(nc.Block())
        before, first, mid, last, after = phases()

        def q_of(slot, h):
            return stack[:, slot, 0, h, :]

        def k_of(slot, h):
            return stack[:, slot, 1, h, :]

        def v_heads(v, c, n, h0=0, nh=HEADS):
            return v[:, c:c + n, h0 * VW:(h0 + nh) * VW].rearrange("p c (h e) -> p c h e", e=VW)

        def tokens(ap):
            return ap.rearrange("(n p) d -> p n d", p=P)

        @block.tensor
        def _(pe):
            mm = nc.tensor.matmul

            def max_scores(ph, i, h, kh):
                hp, kt = divmod(i, KT)
                slot = (hp + 2) % RING
                n = 32 * (GROUPS * ph.b + hp + 2) + 4 * kt + 2 * h + kh
                if (kt, h, kh) == (0, 0, 0):
                    pe.wait_ge(stack_in[slot], 16 * len(BLOCKS) * (2 * ph.b + (hp + 2) // RING + 1))
                wait_past(pe, scores_used, n - 1)
                mm(scores[kh][:, :], q_of(slot, h)[0:STACK, kt * P:(kt + 1) * P],
                   k_of(slot, h)[0:STACK, kh * HALF:(kh + 1) * HALF], start=True, stop=True).then_inc(scores_full, 1)

            def exponents(ph, i, h):
                hp, kt = divmod(i, KT)
                slot = hp % RING
                step = STEPS * ph.b + i
                if (kt, h) == (0, 0):
                    pe.wait_ge(max_loaded, 32 * (GROUPS * ph.b + hp + 1))
                wait_past(pe, exp_done, 2 * step - 1 + h)
                for qh in range(2):
                    one = mm(scoresT[h][:, qh, :], k_of(slot, h)[0:ROWS, kt * P:(kt + 1) * P],
                             q_of(slot, h)[0:ROWS, qh * HALF:(qh + 1) * HALF], start=True, stop=True)
                one.then_inc(scoresT_full, 1)

            def weigh_values(ph, i):
                step = STEPS * ph.b + i - 1
                hp, kt = divmod((i - 1) % STEPS, KT)
                pe.wait_ge(exp_done, 2 * step + 2)
                if kt == 0:
                    wait_past(pe, acc_used, GROUPS * ph.b + hp)
                    pe.wait_ge(v_in[chunk_of(hp)], 16 * (ph.b + 1))
                for h in range(2):
                    for qh in range(2):
                        j = 32 * (2 * h + qh)
                        head = 2 * hp + h
                        one = mm(acc[j:j + 32, :], v_now[:, kt, head * VW:head * VW + 32],
                                 probs[:, (i - 1) % 2, h, qh * HALF:(qh + 1) * HALF],
                                 start=(kt == 0), stop=(kt == KT - 1))
                one.then_inc(pv_done, 1)

            def project_features(src, weight, et, th, more=None):
                pairs = [(s, u, dt) for s, u in [(src, weight)] + ([more] if more else []) for dt in range(DT)]
                for n, (s, u, dt) in enumerate(pairs):
                    one = mm(aux[:, :], w[:, u, dt, et * P:(et + 1) * P], s[:, dt, th * HALF:(th + 1) * HALF],
                             start=(n == 0), stop=(n == len(pairs) - 1))
                return one

            def project_tokens(src, weight, k):
                for c in range(2):
                    for dt in range(DT):
                        t0 = (2 * k + c) * P
                        one = mm(aux_tok[:, c, :], src[:, dt, t0:t0 + P], w[:, weight, dt, :],
                                 start=(dt == 0), stop=(dt == DT - 1))
                return one

            def transpose_tokens(src, k):
                dt, th = divmod(k, 2)
                for c in range(4):
                    one = nc.tensor.transpose(aux[:, c * P:(c + 1) * P], src[:, 4 * th + c, dt * P:(dt + 1) * P],
                                              ident[:, :])
                return one

            def fill(ph, name, k):
                if name == "fin" and k:
                    pe.wait_ge(last_sum, k)
                else:
                    wait_past(pe, aux_used, ph.filled(name, k) - 1)
                if name == "norm":
                    pe.wait_ge(acc_used, GROUPS * ph.b + k)
                    for c in range(4):
                        one = nc.tensor.transpose(aux[:, c * P:(c + 1) * P], o_raw[:, c * P:(c + 1) * P], ident[:, :])
                elif name == "maxT":
                    pe.wait_ge(max_split, GROUPS * ph.b + k + 2)
                    for qt in range(TT):
                        one = nc.tensor.transpose(aux_bf[0:6, qt * P:(qt + 1) * P],
                                                  max_parts[:, qt, :, :].rearrange("p h a -> p (h a)"), ident_bf[:, :])
                elif name == "oT":
                    one = transpose_tokens(o_tok, k)
                elif name == "hT":
                    pe.wait_ge(ln_done[0], ph.b + 2)
                    one = transpose_tokens(xn, k)
                elif name == "h2T":
                    pe.wait_ge(ln_done[1], ph.b)
                    one = transpose_tokens(xn, k)
                elif name in ("q", "k"):
                    one = project_features(hT, WQ if name == "q" else WK, k // 2, k % 2)
                elif name == "v":
                    one = project_tokens(hT, WV, k)
                elif name == "wo":
                    one = project_tokens(fT, WO, k)
                elif name == "gate":
                    th, et, gate = k // 6, k // 3 % 2, k % 3
                    pe.wait_ge(cell_ready, 2 * ph.b)
                    one = project_features(fT, WF + gate, et, th, (cell, UF + gate))
                elif name == "pre":
                    one = project_tokens(fT, WX, k)
                elif name == "fin":
                    pe.wait_ge(cell_ready, 2 * BATCH + 2)
                    one = project_tokens(cell, UO, k)
                elif name == "modT":
                    for m in range(4):
                        for dt in range(DT):
                            for kt in range(DT):
                                c0 = MOD_COLS[m] * D + dt * P
                                o = (m * DT + dt) * BATCH
                                one = mm(aux[:, o:o + BATCH], wmod[:, kt, c0:c0 + P], silu[:, kt, :],
                                         start=(kt == 0), stop=(kt == DT - 1))
                elif name == "mod_rows":
                    for c in range(2):
                        for kt in range(DT):
                            col = (GA, GB)[k // 2] * D
                            one = mm(aux_tok[:, c, :], silu_wide[:, kt, 2 * (k % 2) + c, :], wmod[:, kt, col:col + D],
                                     start=(kt == 0), stop=(kt == DT - 1))
                one.then_inc(aux_full, 1)

            def steps(ph, prior):
                for i in range(STEPS):
                    ahead = ph.qkv or i // KT < GROUPS - 2
                    exponents(ph, i, 0)
                    if ahead:
                        max_scores(ph, i, 0, 0)
                    exponents(ph, i, 1)
                    if ahead:
                        max_scores(ph, i, 0, 1)
                        max_scores(ph, i, 1, 0)
                    if prior or i:
                        weigh_values(ph, i)
                    if ahead:
                        max_scores(ph, i, 1, 1)
                    if i in ph.at:
                        fill(ph, *ph.at[i])

            pe.wait_ge(consts, 1)
            pe.wait_ge(silu_ready, 1)
            pe.wait_ge(mod_in, 32)
            for _, name, k in before.plan:
                if (name, k) == ("q", 0):
                    pe.wait_ge(qkv_in, 80)
                if name == "maxT":
                    break
                fill(before, name, k)
            for i in range(STEPS - 2 * KT, STEPS):
                for h in range(2):
                    for kh in range(2):
                        max_scores(before, i, h, kh)
                if i == STEPS - KT + 1:
                    fill(before, "maxT", GROUPS - 1)
            steps(first, False)
            pe.wait_ge(rest_in, 32)
            with pe.Fori(1, BATCH - 1) as b:
                steps(mid(b), True)
            steps(last, True)
            weigh_values(after, 0)
            for _, name, k in after.plan:
                fill(after, name, k)

        @block.scalar
        def _(act):
            run = nc.scalar.activation

            def exponentials(ph, i):
                step = STEPS * ph.b + i
                wait_past(act, pv_done, step - 1)
                for h in range(2):
                    act.wait_ge(scoresT_full, 2 * step + h + 1)
                    run(probs[:, i % 2, h, :], scoresT[h].rearrange("p a b -> p (a b)"),
                        ACT.Exp).then_inc(exp_done, 1)

            def evacuate_output(ph, k):
                act.wait_ge(pv_done, STEPS * ph.b + KT * k)
                nc.scalar.copy(o_raw[:, :], acc[:, :]).then_inc(acc_used, 1)

            def evacuate(ph, name, k):
                if name not in ("maxT", "oT", "hT", "h2T", "q", "k", "gate"):
                    return
                act.wait_ge(aux_full, ph.filled(name, k))
                dt, th = divmod(k, 2)
                half = slice(th * HALF, (th + 1) * HALF)
                if name == "maxT":
                    wait_past(act, max_loaded, 32 * (GROUPS * ph.b + k + 1))
                    nc.scalar.copy(max_rows[:, :], aux_bf[0:6, :]).then_inc(aux_used, 1)
                elif name == "oT":
                    nc.scalar.copy(fT[:, dt, half], aux[:, :]).then_inc(aux_used, 1)
                elif name == "hT":
                    nb = ph.b + 1
                    alone(act)
                    run(hT[:, dt, half], aux[:, :], ACT.Identity, bias=modT[:, SA, dt, bass.ds(nb, 1)],
                        scale=modT[:, CA, dt, bass.ds(nb, 1)]).then_inc(aux_used, 1)
                elif name == "h2T":
                    t = ph.b - 1
                    alone(act)
                    run(fT[:, dt, half], aux[:, :], ACT.Identity, bias=modT[:, SB, dt, bass.ds(t, 1)],
                        scale=modT[:, CB, dt, bass.ds(t, 1)]).then_inc(aux_used, 1)
                elif name in ("q", "k"):
                    n = k + (4 if name == "k" else 0)
                    wait_past(act, split_done, 8 * (ph.b + 1) + n - 1)
                    run(qk_f32[:, n % 2, :], aux[:, :], ACT.Identity,
                        bias=cols[:, BQ if name == "q" else BK, dt:dt + 1],
                        scale=SCALE if name == "q" else 1.0).then_inc(aux_used, 1)
                elif name == "gate":
                    et, gate, n = k // 3 % 2, k % 3, k // 3
                    if gate == 0 and n >= 2:
                        act.wait_ge(gate_sum, 4 * (ph.b - 1) + n - 1)
                    run(gates[:, n % 2, gate, :], aux[:, :], ACT.Tanh, bias=cols[:, BF + gate, et:et + 1],
                        scale=1.0 if gate == 2 else 0.5).then_inc(aux_used, 1)

            def steps(ph, prior):
                for i in range(STEPS):
                    exponentials(ph, i)
                    if i % KT == 0 and (prior or i):
                        evacuate_output(ph, i // KT)
                    if i in ph.at:
                        evacuate(ph, *ph.at[i])

            act.wait_ge(mod_in, 32)
            run(cs_tanh[:, :, :], cs[:, :, :], ACT.Tanh, scale=0.5).then_inc(cs_tanhed, 1)
            act.wait_ge(mod_seq, 2)
            act.wait_ge(filled_once, 4)
            for _, name, k in before.plan:
                evacuate(before, name, k)
            steps(first, False)
            with act.Fori(1, BATCH - 1) as b:
                steps(mid(b), True)
            steps(last, True)
            evacuate_output(after, 0)
            for _, name, k in after.plan:
                evacuate(after, name, k)
            for k in range(4):
                act.wait_ge(last_sum, k + 1)
                r = result[k % 2]
                run(r[:, :, :, :], r[:, :, :, :], ACT.Tanh).then_inc(last_tanh, 1)

        @block.vector
        def _(dve):
            v = nc.vector

            def maximum(ph, i, h, kh):
                hp, kt = divmod(i, KT)
                n = 32 * (GROUPS * ph.b + hp + 2) + 4 * kt + 2 * h + kh
                dve.wait_ge(scores_full, n + 1)
                col = (2 * kt + h) * 2 + kh
                v.tensor_reduce(max_half[:, hp % 2, col:col + 1], scores[kh][:, :], AX.X,
                                ALU.max).then_inc(scores_used, 1)

            def split_maxima(ph, hp, stage):
                g = GROUPS * ph.b + hp + 1
                if stage == 0:
                    dve.wait_ge(scores_used, 32 * (g + 1))
                    v.tensor_reduce(neg_max[:, :, :], max_half[:, (hp + 1) % 2, :].rearrange(
                        "p (q h k) -> p q h k", h=2, k=2), AX.X, ALU.max, negate=True).then_inc(max_seq, 1)
                elif stage == 1:
                    dve.wait_ge(max_seq, 4 * g + 1)
                    wait_past(dve, max_loaded, 32 * g)
                    v.tensor_copy(max_parts[:, :, :, 0], neg_max[:, :, :]).then_inc(max_seq, 1)
                    dve.wait_ge(max_seq, 4 * g + 2)
                    v.tensor_tensor(max_rest[:, :, :], neg_max[:, :, :], max_parts[:, :, :, 0],
                                    ALU.subtract).then_inc(max_seq, 1)
                else:
                    dve.wait_ge(max_seq, 4 * g + 3)
                    v.tensor_copy(max_parts[:, :, :, 1], max_rest[:, :, :]).then_inc(max_seq, 1)
                    dve.wait_ge(max_seq, 4 * g + 4)
                    v.tensor_tensor(max_parts[:, :, :, 2], max_rest[:, :, :], max_parts[:, :, :, 1],
                                    ALU.subtract).then_inc(max_split, 1)

            def norm_stats(which, src, tiles):
                for n in tiles:
                    one = v.bn_stats(stats[:, which, n, :], src[:, n, :])
                if tiles[-1] == TT - 1:
                    one.then_inc(ln_seq[which], 1)

            def norm_moments(which, n):
                dve.wait_ge(ln_seq[which], 2 * n + 1)
                alone(dve)
                for t in range(TT):
                    one = v.bn_aggr(mean_var[:, which, t, :], stats[:, which, t, :])
                one.then_inc(ln_seq[which], 1)
                dve.wait_ge(ln_seq[which], 2 * n + 2)
                v.tensor_scalar(var_eps[:, which, :], mean_var[:, which, :, 1], EPS, None,
                                ALU.add).then_inc(var_ready[which], 1)

            def norm_apply(which, n, src, tiles):
                dve.wait_ge(rstd_ready[which], n + 1)
                for t in tiles:
                    one = v.tensor_scalar(xn[:, t, :], src[:, t, :], mean_var[:, which, t, 0:1],
                                          rstd[:, which, t:t + 1], ALU.subtract, ALU.mult)
                if tiles[-1] == TT - 1:
                    one.then_inc(ln_done[which], 1)

            def sum_gates(ph, n):
                th, et = divmod(n, 2)
                half = slice(th * HALF, (th + 1) * HALF)
                f, i, g = (gates[:, n % 2, m, :] for m in range(GATES))
                m = 4 * (ph.b - 1) + n
                dve.wait_ge(aux_used, ph.filled("gate", 3 * n + 2))
                dve.wait_ge(cell_ready, 2 * ph.b + th)
                v.scalar_tensor_tensor(f, f, 1.0, cell[:, et, half], ALU.add, ALU.mult).then_inc(gate_seq, 1)
                v.scalar_tensor_tensor(i, i, 1.0, g, ALU.add, ALU.mult).then_inc(gate_seq, 1)
                dve.wait_ge(gate_seq, 2 * m + 2)
                v.tensor_tensor(cell_sum[:, et, :], f, i, ALU.add).then_inc(gate_sum, 1)

            def evacuate(ph, name, k):
                if name not in ("norm", "v", "wo", "pre"):
                    return
                dve.wait_ge(aux_full, ph.filled(name, k))
                if name == "norm":
                    hp = (k - 1) % GROUPS
                    o = aux.rearrange("p (c j e) -> p c j e", c=4, j=4)
                    v.reciprocal(inv_sum[:, :, :], o[:, :, :, DK]).then_inc(sums_inverted, 1)
                    dve.wait_ge(sums_inverted, GROUPS * ph.b + k)
                    for h in range(2):
                        head = 2 * hp + h
                        one = v.tensor_tensor(
                            o_tok.rearrange("p (q c) d -> p q c d", q=2)[:, :, :, head * DK:(head + 1) * DK],
                            o.rearrange("p c j e -> p j c e")[:, 2 * h:2 * h + 2, :, 0:DK],
                            inv_sum.rearrange("p c j -> p j c")[:, 2 * h:2 * h + 2, :].unsqueeze(3).to_broadcast(
                                [P, 2, 4, DK]), ALU.mult)
                    one.then_inc(aux_used, 1)
                elif name == "v":
                    wait_past(dve, v_in[-1], 16 * (ph.b + 1))
                    bias = rows[:, BV, :].rearrange("p (h d) -> p h d", d=DK).unsqueeze(1).to_broadcast(
                        [P, 2, HEADS, DK])
                    one = v.tensor_tensor(v_heads(v_next, 2 * k, 2)[:, :, :, 0:DK],
                                          aux.rearrange("p (c h d) -> p c h d", c=2, d=DK), bias, ALU.add)
                    if k == 0:
                        one.then_inc(v_added, 1)
                        dve.wait_ge(v_added, ph.b + 2)
                        first_key = v_heads(v_next, 0, 1)[0:1, 0, :, 0:DK]
                        one = v.tensor_scalar(first_key, first_key, 0.5, None, ALU.mult)
                    one.then_inc(aux_used, 1)
                elif name == "wo":
                    t = ph.b - 1
                    if k >= 2:
                        dve.wait_ge(x1_ready, 4 * t + k - 1)
                    v.tensor_tensor(attn[:, k % 2, :, :], aux_tok[:, :, :], mod_rows[:, 0, bass.ds(t, 1), :].to_broadcast(
                        [P, 2, D]), ALU.mult).then_inc(aux_used, 1)
                elif name == "pre":
                    t = ph.b - 1
                    if k >= 2:
                        dve.wait_ge(pre_out[k % 2], 16 * (2 * t + 1))
                    v.tensor_tensor(pre[:, k % 2, :, :], aux_tok[:, :, :], rows[:, BH:BH + 1, :].to_broadcast(
                        [P, 2, D]), ALU.add).then_inc(aux_used, 1)

            def stats_after_attention(ph, k):
                dve.wait_ge(x1_ready, 4 * (ph.b - 1) + k + 1)
                norm_stats(1, x1, [2 * k, 2 * k + 1])

            def steps(ph):
                for i in range(STEPS):
                    hp, kt = divmod(i, KT)
                    if kt < 3 and (ph.qkv or hp < GROUPS - 1):
                        split_maxima(ph, hp, kt)
                    if ph.qkv or hp < GROUPS - 2:
                        for h in range(2):
                            for kh in range(2):
                                maximum(ph, i, h, kh)
                    if i in ph.at:
                        evacuate(ph, *ph.at[i])
                    if ph.qkv and i == 4:
                        dve.wait_ge(xn_in, 16 * (ph.b + 2))
                    if ph.qkv and 4 <= i < 8:
                        norm_stats(0, xn, [2 * (i - 4), 2 * (i - 4) + 1])
                    if ph.qkv and i == 8:
                        norm_moments(0, ph.b + 1)
                    if ph.qkv and i in (10, 11):
                        norm_apply(0, ph.b + 1, xn, list(range(4 * (i - 10), 4 * (i - 10) + 4)))
                    if ph.post and 14 <= i < 18:
                        stats_after_attention(ph, i - 14)
                    if ph.post and i == 18:
                        norm_moments(1, ph.b - 1)
                    if ph.post and i in (20, 21):
                        if ph.qkv:
                            dve.wait_ge(aux_used, ph.filled("hT", 3))
                        norm_apply(1, ph.b - 1, x1, list(range(4 * (i - 20), 4 * (i - 20) + 4)))
                    name, k = ph.at.get(i - 1, (None, 0))
                    if name == "gate" and k % 3 == 2:
                        sum_gates(ph, k // 3)

            v.memset(v_next[:, :, :], 1.0)
            v.memset(v_now[:, :, :], 1.0)
            v.memset(stack[STACK:ROWS, :, 1, :, :], 1.0).then_inc(filled_once, 1)
            dve.wait_ge(mod_in, 32)
            dve.wait_ge(cs_tanhed, 1)
            v.scalar_tensor_tensor(silu[:, :, :], cs_tanh[:, :, :], 1.0, cs[:, :, :], ALU.add,
                                   ALU.mult).then_inc(filled_once, 1)
            dve.wait_ge(filled_once, 2)
            v.tensor_scalar(silu[:, :, :], silu[:, :, :], 0.5, None, ALU.mult).then_inc(filled_once, 1)
            dve.wait_ge(filled_once, 3)
            v.tensor_copy(silu_wide[:, :, :, :], silu[:, :, :].unsqueeze(3).to_broadcast(
                [P, DT, BATCH, P])).then_inc(silu_ready, 1)
            dve.wait_ge(xn_in, 16)
            norm_stats(0, xn, list(range(TT)))
            norm_moments(0, 0)
            dve.wait_ge(qkv_in, 80)
            v.tensor_scalar(cols[:, BQ, :], cols[:, BQ, :], SCALE, None, ALU.mult)
            v.tensor_scalar(cols[:, BF:BI + 1, :], cols[:, BF:BI + 1, :], 0.5, None, ALU.mult).then_inc(filled_once, 1)
            dve.wait_ge(aux_full, before.filled("modT", 0))
            v.tensor_copy(modT.rearrange("p m t b -> p (m t b)"), aux[:, 0:4 * DT * BATCH]).then_inc(aux_used, 1)
            dve.wait_ge(aux_used, before.filled("modT", 0))
            v.tensor_scalar(modT[:, CA, :, :], modT[:, CA, :, :], 1.0, None, ALU.add).then_inc(mod_seq, 1)
            v.tensor_scalar(modT[:, CB, :, :], modT[:, CB, :, :], 1.0, None, ALU.add).then_inc(mod_seq, 1)
            norm_apply(0, 0, xn, list(range(TT)))
            for k in range(4):
                dve.wait_ge(aux_full, before.filled("mod_rows", k))
                b0 = 2 * (k % 2)
                v.tensor_copy(mod_rows[:, k // 2, b0:b0 + 2, :], aux_tok[:, :, :]).then_inc(aux_used, 1)
            dve.wait_ge(aux_used, before.filled("mod_rows", 3))
            v.tensor_scalar(mod_sign[:, :, :, :], mod_rows[:, :, :, :], 0.0, 2.0, ALU.is_ge, ALU.mult).then_inc(mod_seq, 1)
            dve.wait_ge(mod_seq, 3)
            v.tensor_scalar(mod_sign[:, :, :, :], mod_sign[:, :, :, :], -1.0, None, ALU.add).then_inc(mod_seq, 1)
            dve.wait_ge(mod_seq, 4)
            v.tensor_tensor(mod_rows[:, :, :, :], mod_rows[:, :, :, :], mod_sign[:, :, :, :], ALU.mult).then_inc(mod_seq, 1)
            dve.wait_ge(mod_seq, 5)
            v.scalar_tensor_tensor(mod_rows.rearrange("p a b d -> p (a b d)"), mod_rows.rearrange("p a b d -> p (a b d)"),
                                   0.25, mod_sign.rearrange("p a b d -> p (a b d)"), ALU.max,
                                   ALU.mult).then_inc(mod_seq, 1)
            dve.wait_ge(mod_seq, 6)
            v.tensor_tensor(ga_bo, mod_rows[:, 0, :, :], rows[:, BO:BO + 1, :].to_broadcast([P, BATCH, D]),
                            ALU.mult).then_inc(mod_ready, 1)
            for et in range(DT):
                v.tensor_copy(cell[:, et, :], cols[:, C0, et:et + 1].to_broadcast([P, L])).then_inc(cell_ready, 1)
            for k in range(4):
                evacuate(before, "v", k)
            for i in range(STEPS - 2 * KT, STEPS):
                hp, kt = divmod(i, KT)
                if hp == GROUPS - 1 and kt == 0:
                    for stage in range(3):
                        split_maxima(before, hp, stage)
                for h in range(2):
                    for kh in range(2):
                        maximum(before, i, h, kh)
            steps(first)
            with dve.Fori(1, BATCH - 1) as b:
                steps(mid(b))
            steps(last)
            for _, name, k in after.plan:
                evacuate(after, name, k)
                if name == "wo":
                    stats_after_attention(after, k)
                if (name, k) == ("wo", 3):
                    norm_moments(1, BATCH - 1)
                    norm_apply(1, BATCH - 1, x1, list(range(TT)))
                if name == "gate" and k % 3 == 2:
                    sum_gates(after, k // 3)
            dve.wait_ge(pre_in, 16 * BATCH)
            for k in range(5):
                if k < 4:
                    dve.wait_ge(aux_full, after.filled("fin", k))
                    if k >= 2:
                        dve.wait_ge(out_done[k % 2], 16 * BATCH)
                    v.tensor_tensor(result[k % 2].rearrange("p t n d -> p t (n d)"),
                                    aux.unsqueeze(1).to_broadcast([P, BATCH, HALF]),
                                    pre_all[:, :, 2 * k:2 * k + 2, :].rearrange("p t n d -> p t (n d)"),
                                    ALU.add).then_inc(last_sum, 1)
                if k:
                    dve.wait_ge(last_tanh, k)
                    r = result[(k - 1) % 2]
                    gb = mod_rows[:, 1, :, :].unsqueeze(2).to_broadcast([P, BATCH, 2, D])
                    v.tensor_tensor(r[:, :, :, :], r[:, :, :, :], gb, ALU.mult).then_inc(last_gated, 1)

        @block.gpsimd
        def _(pool):
            g = nc.gpsimd

            def split(ph, name, k):
                n = k + (4 if name == "k" else 0)
                m = 8 * (ph.b + 1) + n
                pool.wait_ge(aux_used, ph.filled(name, k))
                wait_past(pool, parts_out[n % 2], 16 * (4 * (ph.b + 1) + n // 2))
                alone(pool)
                whole = qk_f32[:, n % 2, :]
                part = [parts[:, n % 2, c, :] for c in range(3)]
                g.tensor_scalar(part[0], whole, 1.0, 0.0, ALU.mult, ALU.add).then_inc(split_seq, 1)
                pool.wait_ge(split_seq, 3 * m + 1)
                g.tensor_tensor(rest[:, :], whole, part[0], ALU.subtract).then_inc(split_seq, 1)
                pool.wait_ge(split_seq, 3 * m + 2)
                alone(pool)
                g.tensor_scalar(part[1], rest[:, :], 1.0, 0.0, ALU.mult, ALU.add).then_inc(split_seq, 1)
                pool.wait_ge(split_seq, 3 * m + 3)
                g.tensor_tensor(part[2], rest[:, :], part[1], ALU.subtract).then_inc(split_done, 1)

            def inverse_deviation(which, n):
                pool.wait_ge(var_ready[which], n + 1)
                g.tensor_tensor(rstd[:, which, :], var_eps[:, which, :], minus_half[:, :],
                                ALU.pow).then_inc(rstd_ready[which], 1)

            def bias_residual(ph):
                t = ph.b - 1
                pool.wait_ge(res_in, 16 * ph.b)
                g.tensor_tensor(x1[:, :, :], x1[:, :, :], ga_bo[:, bass.ds(t, 1), :].to_broadcast([P, TT, D]),
                                ALU.add).then_inc(res_biased, 1)

            def add_residual(ph, k):
                pool.wait_ge(aux_used, ph.filled("wo", k))
                pool.wait_ge(res_biased, ph.b)
                two = x1[:, 2 * k:2 * k + 2, :]
                g.tensor_tensor(two, attn[:, k % 2, :, :], two, ALU.add).then_inc(x1_ready, 1)

            def halve_cell(ph, th):
                pool.wait_ge(gate_sum, 4 * (ph.b - 1) + 2 * th + 2)
                alone(pool)
                g.tensor_scalar(cell[:, :, th * HALF:(th + 1) * HALF], cell_sum[:, :, :], 0.5, 0.0, ALU.mult,
                                ALU.add).then_inc(cell_ready, 1)

            def steps(ph):
                for i in range(STEPS):
                    name, k = ph.at.get(i, (None, 0))
                    if ph.post and i == 1:
                        bias_residual(ph)
                    if name in ("q", "k"):
                        split(ph, name, k)
                    if name == "wo":
                        add_residual(ph, k)
                    if ph.qkv and i == 8:
                        inverse_deviation(0, ph.b + 1)
                    if ph.post and i == 18:
                        inverse_deviation(1, ph.b - 1)
                    name, k = ph.at.get(i - 1, (None, 0))
                    if name == "gate" and k % 6 == 5:
                        halve_cell(ph, k // 6)

            g.memset(ident[:, :], 0.0)
            g.memset(ident_bf[:, :], 0.0)
            g.memset(minus_half[:, :], -0.5).then_inc(zeros, 1)
            pool.wait_ge(zeros, 1)
            g.affine_select(out=ident[:, :], in_=ident[:, :], compare_op=ALU.not_equal, fill=1.0, base=0,
                            pattern=[[-1, P]], channel_multiplier=1)
            g.affine_select(out=ident_bf[:, :], in_=ident_bf[:, :], compare_op=ALU.not_equal, fill=1.0, base=0,
                            pattern=[[-1, P]], channel_multiplier=1).then_inc(consts, 1)
            inverse_deviation(0, 0)
            for _, name, k in before.plan:
                if name in ("q", "k"):
                    split(before, name, k)
            pool.wait_ge(mod_ready, 1)
            steps(first)
            with pool.Fori(1, BATCH - 1) as b:
                steps(mid(b))
            steps(last)
            bias_residual(after)
            for _, name, k in after.plan:
                if name == "wo":
                    add_residual(after, k)
                if (name, k) == ("wo", 3):
                    inverse_deviation(1, BATCH - 1)
                if name == "gate" and k % 6 == 5:
                    halve_cell(after, k // 6)
            for k in range(4):
                pool.wait_ge(last_gated, k + 1)
                pool.wait_ge(x1_in[k % 2], 16 * BATCH * (k // 2 + 1))
                r = result[k % 2]
                g.tensor_tensor(r[:, :, :, :], r[:, :, :, :], x1_chunk[:, k % 2], ALU.add).then_inc(result_ready, 1)

        @block.sync
        def _(sp):
            def load_stack(ph, hp):
                nb, h3 = (ph.b, hp + 3) if hp + 3 < GROUPS else (ph.b + 1, hp + 3 - GROUPS)
                slot = (hp + 3) % RING
                if hp + 3 == GROUPS:
                    for n in range(2):
                        sp.wait_ge(parts_out[n], 64 * (ph.b + 2))
                wait_past(sp, scoresT_full, 2 * KT * (GROUPS * ph.b + hp))
                alone(sp)
                part_of = pieces[bass.ds(nb, 1)].rearrange("o k c (g h d) t -> (o k) c g h d t", g=GROUPS, h=2)
                for block, qk, part in BLOCKS:
                    r = block * DK
                    sp.dma_start(stack[r:r + DK, slot, qk, :, :], part_of[qk, part, h3].rearrange(
                        "h d t -> d h t")).then_inc(stack_in[slot], 16)

            def move_values(c, batch, groups_done):
                lo, hi = V_CHUNKS[c]
                wait_past(sp, pv_done, KT * groups_done)
                a, z = 2 * lo * VW, 2 * (hi + 1) * VW
                sp.dma_start(v_now[:, :, a:z], v_next[:, :, a:z]).then_inc(v_in[c], 16)

            def place_maxima(ph, hp):
                slot = (hp + 1) % RING
                sp.wait_ge(aux_used, ph.filled("maxT", hp))
                for h in range(2):
                    sp.dma_start(stack[STACK:ROWS, slot, 0, h, :], max_rows[3 * h:3 * h + 3, :]).then_inc(max_loaded, 16)

            def store_parts(ph, name, k):
                n = k + (4 if name == "k" else 0)
                et, th = divmod(k, 2)
                sp.wait_ge(split_done, 8 * (ph.b + 1) + n + 1)
                alone(sp)
                dst = pieces[bass.ds(ph.b + 1, 1), n // 4, :, et * P:(et + 1) * P, th * HALF:(th + 1) * HALF]
                sp.dma_start(dst.rearrange("o c p t -> p (o c) t"), parts[:, n % 2, :, :]).then_inc(parts_out[n % 2], 16)

            def load_residual(ph):
                sp.wait_ge(aux_used, ph.base)
                alone(sp)
                sp.dma_start(x1[:, :, :], tokens(x[bass.ds(ph.b - 1, 1)].rearrange("o n d -> (o n) d"))).then_inc(res_in, 16)

            def store_pre(ph, k):
                t = ph.b - 1
                sp.wait_ge(aux_used, ph.filled("pre", k))
                alone(sp)
                sp.dma_start(pre_spill[:, bass.ds(t, 1), 2 * k:2 * k + 2, :].rearrange("p o n d -> p (o n) d"),
                             pre[:, k % 2, :, :]).then_inc(pre_out[k % 2], 16)

            def store_x1(ph):
                sp.wait_ge(x1_ready, 4 * ph.b)
                alone(sp)
                sp.dma_start(x1_spill[:, bass.ds(ph.b - 1, 1), :, :].rearrange("p o n d -> p (o n) d"),
                             x1[:, :, :]).then_inc(x1_out, 16)

            def store_result(k):
                sp.wait_ge(result_ready, k + 1)
                for t in range(BATCH):
                    sp.dma_start(tokens(out[t])[:, 2 * k:2 * k + 2, :], result[k % 2][:, t]).then_inc(out_done[k % 2], 16)

            def spilled(ph):
                sp.wait_ge(x1_out, 16 * ph.b)
                alone(sp)
                for n in range(2):
                    sp.wait_ge(pre_out[n], 32 * ph.b)
                    alone(sp)

            def steps(ph):
                for i in range(STEPS):
                    hp, kt = divmod(i, KT)
                    if kt == 4 and (ph.qkv or hp < GROUPS - 1):
                        place_maxima(ph, hp)
                    if i == 0 and ph.qkv:
                        sp.wait_ge(aux_used, ph.base)
                        alone(sp)
                        sp.dma_start(xn[:, :, :], tokens(x[bass.ds(ph.b + 1, 1)].rearrange("o n d -> (o n) d"))
                                     ).then_inc(xn_in, 16)
                    if i == 0 and ph.post:
                        load_residual(ph)
                    if kt == 0 and (ph.qkv or hp + 3 < GROUPS):
                        load_stack(ph, hp)
                    if i == 1:
                        move_values(3, ph.b, GROUPS * ph.b)
                    if kt == 1 and hp >= 5 and ph.qkv:
                        move_values(hp - 5, ph.b + 1, GROUPS * ph.b + V_CHUNKS[hp - 5][1] + 1)
                    name, k = ph.at.get(i - 1, (None, 0))
                    if name in ("q", "k"):
                        store_parts(ph, name, k)
                    if name == "pre":
                        store_pre(ph, k)
                    if ph.post and i == 18:
                        store_x1(ph)
                    if ph.post and i == STEPS - 1:
                        spilled(ph)

            sp.dma_start(cs[:, :, :], cT.rearrange("(t p) b -> p t b", p=P)).then_inc(mod_in, 16)
            sp.dma_start(xn[:, :, :], tokens(x[0])).then_inc(xn_in, 16)
            sp.dma_start(wmod, wmod_in.rearrange("(t p) n -> p t n", p=P)).then_inc(mod_in, 16)
            sp.dma_start(cols[:, :, :], cols_in).then_inc(qkv_in, 16)
            for n in range(3):
                sp.dma_start(rows[:, n, :], rows_in[n].partition_broadcast(P)).then_inc(qkv_in, 16)
            sp.dma_start(w[:, WQ:WV + 1, :, :], w_all[:, WQ:WV + 1, :, :]).then_inc(qkv_in, 16)
            sp.dma_start(w[:, WO:WX + 1, :, :], w_all[:, WO:WX + 1, :, :]).then_inc(rest_in, 16)
            sp.dma_start(w[:, UF:UO + 1, :, :], w_all[:, UF:UO + 1, :, :]).then_inc(rest_in, 16)
            for _, name, k in before.plan:
                if name in ("q", "k"):
                    store_parts(before, name, k)
            sp.wait_ge(filled_once, 1)
            for hp in (5, 6, 7):
                load_stack(before, hp)
            sp.wait_ge(aux_used, before.filled("v", 3))
            for c in range(3):
                move_values(c, 0, 0)
            place_maxima(before, GROUPS - 1)
            steps(first)
            with sp.Fori(1, BATCH - 1) as b:
                steps(mid(b))
            steps(last)
            load_residual(after)
            for k in range(4):
                if k == 0:
                    store_x1(after)
                store_pre(after, k)
            spilled(after)
            for t in range(BATCH):
                sp.dma_start(pre_all[:, t], pre_spill[:, t]).then_inc(pre_in, 16)
            for k in range(4):
                if k >= 2:
                    sp.wait_ge(result_ready, k - 1)
                for t in range(BATCH):
                    sp.dma_start(x1_chunk[:, k % 2, t], x1_spill[:, t, 2 * k:2 * k + 2, :]).then_inc(x1_in[k % 2], 16)
                if k >= 1:
                    store_result(k - 1)
            store_result(3)
            for n in range(2):
                sp.wait_ge(out_done[n], 16 * 2 * BATCH)

    return nc


def kernel(**inputs):
    import numpy as np
    import concourse.bacc as bacc
    from concourse.bass_utils import run_bass_kernel_spmd as run

    a = {name: np.asarray(v) for name, v in inputs.items()}
    matrices = [a[f"L0_attn_W{n}"] for n in "qkvo"] + [a[f"L0_ffn_{n}"] for n in
                                                      ("wf", "wi", "wc", "wo", "uf", "ui", "uc", "uo")]
    columns = [a["L0_attn_bq"], a["L0_attn_bk"], a["L0_ffn_bf"], a["L0_ffn_bi"], a["L0_ffn_bc"], a["L0_ffn_in_c"]]
    arrays = {
        "x": a["L0_attn_x"],
        "w_all": np.stack(matrices).transpose(2, 0, 1).reshape(DT, P, 12, D).transpose(1, 2, 0, 3),
        "cols": np.stack(columns).reshape(6, DT, P).transpose(2, 0, 1),
        "rows": np.stack([a["L0_attn_bv"], a["L0_attn_bo"], a["L0_ffn_bo"]]),
        "cT": a["L0_c"].T,
        "wmod": a["L0_wmod"],
    }
    arrays = {n: np.ascontiguousarray(v) for n, v in arrays.items()}
    nc = bacc.Bacc("TRN2", target_bir_lowering=False, num_devices=1)
    args = [nc.dram_tensor(f"in_{n}", v.shape, mybir.dt.from_np(v.dtype), kind="ExternalInput").ap() for n, v in arrays.items()]
    args += [nc.dram_tensor("pieces", (BATCH, 2, 3, D, L), BF16, kind="Internal").ap(),
             nc.dram_tensor("x1_spill", (P, BATCH, TT, D), F32, kind="Internal").ap(),
             nc.dram_tensor("pre_spill", (P, BATCH, TT, D), F32, kind="Internal").ap()]
    args.append(nc.dram_tensor("y", (BATCH, L, D), F32, kind="ExternalOutput").ap())
    adaln_layer(nc, *args)
    r = run(nc, [{f"in_{n}": v for n, v in arrays.items()}], core_ids=[0])
    return r.results[0]["y"]
```

```python
from contextlib import ExitStack

import concourse.bass as bass
from concourse import mybir

F32 = mybir.dt.float32
BF16 = mybir.dt.bfloat16
ALU = mybir.AluOpType
ACT = mybir.ActivationFunctionType
AX = mybir.AxisListType

P = 128
BATCH, L, D = 4, 1024, 256
HEADS = 16
DK = D // HEADS
DT = D // P
TT = L // P
HALF = L // 2
GROUPS = HEADS // 2
KT = L // P
STEPS = GROUPS * KT
RING = 4
STACK = 6 * DK
ROWS = STACK + 3
VW = DK + 1
VPITCH = HEADS * VW + 16
SCALE = DK ** -0.5
EPS = 1e-5
GATES = 3

WQ, WK, WV, WO, WF, WI, WC, WX, UF, UI, UC, UO = range(12)
BQ, BK, BF, BI, BC, C0 = range(6)
BV, BO, BH = range(3)
SA, CA, SB, CB = range(4)
MOD_COLS = (0, 1, 3, 4)
GA, GB = 2, 5

PRODUCTS = ((0, 0), (0, 1), (0, 2), (1, 0), (1, 1), (2, 0))
BLOCKS = [(n, qk, product[qk]) for n, product in enumerate(PRODUCTS) for qk in range(2)]

V_CHUNKS = ((0, 4), (5, 5), (6, 6), (7, 7))


def chunk_of(hp):
    return max(0, hp - 4)


BY_ACT = ("maxT", "oT", "hT", "h2T", "qk", "gate")


class Phase:

    QKV = [("hT", 4), ("qk", 8), ("v", 4)]
    POST = [("oT", 4), ("wo", 4)]
    FFN = [("h2T", 4), ("gate", 12), ("pre", 4)]

    def __init__(self, b, base, qkv, post, plan=None):
        self.b, self.base, self.qkv, self.post = b, base, qkv, post
        self.by_turns = plan is not None
        self.plan = self.of_steps() if plan is None else plan
        self.order, n = {}, [0, 0]
        for _, name, k in self.plan:
            self.order[name, k] = tuple(n)
            n[name in BY_ACT] += 1
        self.size = tuple(n)
        self.at = {step: (name, k) for step, name, k in self.plan}

    def of_steps(self):
        free = [i for i in range(STEPS) if i % KT not in (2, 3)]
        dense = [(n, k) for n, c in self.POST + self.QKV + self.FFN for k in range(c)]
        of_next = [n for n, _ in self.QKV]
        plan = []
        for i, (name, k) in zip(free[2:], dense):
            if self.qkv if name in of_next else self.post:
                plan.append((i, name, k))
        for hp in range(GROUPS):
            if self.post or hp:
                plan.append((hp * KT + 2, "norm", hp))
            if self.qkv or hp < GROUPS - 1:
                plan.append((hp * KT + 3, "maxT", hp))
        return sorted(plan)

    def full(self, name, k):
        return sum(self.base) + sum(self.order[name, k]) + 1

    def read(self, name, k):
        who = name in BY_ACT
        return self.base[who] + self.order[name, k][who] + 1

    def end(self):
        return self.base[0] + self.size[0], self.base[1] + self.size[1]


def planned(*parts):
    return [(None, name, k) for name, ks in parts for k in ks]


PROLOGUE = planned(("modT", [0]), ("hT", range(4)), ("qk", range(4)), ("v", range(4)), ("qk", range(4, 8)),
                   ("mod_rows", range(4)), ("maxT", [GROUPS - 1]))
TAIL = planned(("norm", [0]), ("oT", range(4)), ("wo", range(4)), ("h2T", [0, 1]), ("gate", range(6)),
               ("pre", [0, 1]), ("h2T", [2, 3]), ("fin", [0, 1]), ("gate", range(6, 12)), ("pre", [2, 3]),
               ("fin", [2, 3]))


def phases():
    before = Phase(-1, (0, 0), True, False, PROLOGUE)
    first = Phase(0, before.end(), True, False)
    start, size = first.end(), Phase(1, (0, 0), True, True).size

    def between(b):
        return start[0] + (b - 1) * size[0], start[1] + (b - 1) * size[1]

    def mid(b):
        return Phase(b, between(b), True, True)

    last = Phase(BATCH - 1, between(BATCH - 1), False, True)
    after = Phase(BATCH, last.end(), False, True, TAIL)
    return before, first, mid, last, after


def wait_past(eng, sem, value):
    if not isinstance(value, int) or value > 0:
        eng.wait_ge(sem, value)


def adaln_layer(nc, x, w_all, cols_in, rows_in, cT, wmod_in, pieces, x1_spill, pre_spill, out):
    ctx = ExitStack()
    with ctx:
        def sb(name, shape, dt=F32):
            return ctx.enter_context(nc.sbuf_tensor(name, shape, dt))[:]

        def pb(name, shape, dt=F32):
            return ctx.enter_context(nc.psum_tensor(name, shape, dt))[:]

        def sem(name):
            return ctx.enter_context(nc.semaphore(name))

        stack = sb("stack", [P, RING, 2, 2, L], BF16)
        probs = sb("probs", [P, 2, 2, L])
        v_now = sb("v_now", [P, KT, VPITCH])
        v_next = sb("v_next", [P, KT, VPITCH])
        w = sb("w", [P, 12, DT, D])
        cols = sb("cols", [P, 6, DT])
        rows = sb("rows", [P, 3, D])
        xn = sb("xn", [P, TT, D])
        x1 = sb("x1", [P, TT, D])
        o_tok = sb("o_tok", [P, TT, D])
        hT = sb("hT", [P, DT, L])
        fT = sb("fT", [P, DT, L])
        cell = sb("cell", [P, DT, L])
        cell_sum = sb("cell_sum", [P, DT, HALF])
        gates = sb("gates", [P, 2, GATES, HALF])
        qk_f32 = sb("qk_f32", [P, 2, HALF])
        rest = sb("rest", [P, HALF])
        parts = sb("parts", [P, 2, 3, HALF], BF16)
        attn = sb("attn", [P, 2, 2, D])
        pre = sb("pre", [P, 2, 2, D])
        o_raw = sb("o_raw", [P, HALF])
        inv_sum = sb("inv_sum", [P, 4, 4])
        max_half = sb("max_half", [P, 2, 2 * TT * 2])
        neg_max = sb("neg_max", [P, TT, 2])
        max_rest = sb("max_rest", [P, TT, 2])
        max_parts = sb("max_parts", [P, TT, 2, 3], BF16)
        max_rows = sb("max_rows", [6, L], BF16)
        cs = sb("cs", [P, DT, BATCH])
        cs_tanh = sb("cs_tanh", [P, DT, BATCH])
        silu = sb("silu", [P, DT, BATCH])
        silu_wide = sb("silu_wide", [P, DT, BATCH, P])
        modT = sb("modT", [P, 4, DT, BATCH])
        mod_rows = sb("mod_rows", [P, 2, BATCH, D])
        mod_sign = sb("mod_sign", [P, 2, BATCH, D])
        ga_bo = mod_sign[:, 0]
        stats = sb("stats", [P, 2, TT, 6])
        mean_var = sb("mean_var", [P, 2, TT, 2])
        var_eps = sb("var_eps", [P, 2, TT])
        rstd = sb("rstd", [P, 2, TT])
        minus_half = sb("minus_half", [P, TT])
        ident = sb("ident", [P, P])
        ident_bf = sb("ident_bf", [P, P], BF16)
        wmod = probs.rearrange("p a h l -> p (a h l)")[:, 0:DT * 6 * D].rearrange("p (t n) -> p t n", t=DT)
        pre_all = stack.rearrange("p s k h l -> p (s k h l)").bitcast(F32).rearrange(
            "p (t n d) -> p t n d", t=BATCH, d=D)
        x1_chunk = probs.rearrange("p a h l -> p a (h l)").rearrange("p a (t n d) -> p a t n d", t=BATCH, d=D)
        result = [xn.rearrange("p (t n) d -> p t n d", t=BATCH),
                  hT.rearrange("p a l -> p (a l)").rearrange("p (t n d) -> p t n d", t=BATCH, d=D)]

        scoresT = [pb(f"scoresT{h}", [P, 2, HALF]) for h in range(2)]
        scores = [pb(f"scores{i}", [P, HALF]) for i in range(2)]
        acc = pb("acc", [P, HALF])
        aux = pb("aux", [P, HALF])
        turns = [aux, scoresT[0][:, 0, :], scoresT[0][:, 1, :], scoresT[1][:, 0, :], scoresT[1][:, 1, :],
                 scores[0], scores[1]]

        mod_in = sem("mod_in")
        qkv_in = sem("qkv_in")
        rest_in = sem("rest_in")
        xn_in = sem("xn_in")
        res_in = sem("res_in")
        waited = sem("waited")
        zeros = sem("zeros")
        consts = sem("consts")
        filled_once = sem("filled_once")
        mod_seq = sem("mod_seq")
        cs_tanhed = sem("cs_tanhed")
        silu_ready = sem("silu_ready")
        mod_ready = sem("mod_ready")
        scoresT_full = sem("scoresT_full")
        exp_done = sem("exp_done")
        pv_done = sem("pv_done")
        acc_used = sem("acc_used")
        scores_full = sem("scores_full")
        scores_used = sem("scores_used")
        max_seq = sem("max_seq")
        max_split = sem("max_split")
        max_loaded = sem("max_loaded")
        full = sem("full")
        act_read = sem("act_read")
        dve_read = sem("dve_read")
        sums_inverted = sem("sums_inverted")
        stack_in = [sem(f"stack_in{s}") for s in range(RING)]
        v_in = [sem(f"v_in{c}") for c in range(len(V_CHUNKS))]
        v_added = sem("v_added")
        stats_ready = [sem(f"stats_ready{n}") for n in range(2)]
        mean_ready = [sem(f"mean_ready{n}") for n in range(2)]
        var_ready = [sem(f"var_ready{n}") for n in range(2)]
        rstd_ready = [sem(f"rstd_ready{n}") for n in range(2)]
        ln_done = [sem(f"ln_done{n}") for n in range(2)]
        split_seq = sem("split_seq")
        split_done = sem("split_done")
        parts_out = [sem(f"parts_out{n}") for n in range(2)]
        res_biased = sem("res_biased")
        attn_ready = sem("attn_ready")
        x1_ready = sem("x1_ready")
        x1_out = sem("x1_out")
        pre_ready = sem("pre_ready")
        pre_out = [sem(f"pre_out{n}") for n in range(2)]
        gate_seq = sem("gate_seq")
        gate_sum = sem("gate_sum")
        cell_ready = sem("cell_ready")
        pre_in = sem("pre_in")
        x1_in = [sem(f"x1_in{n}") for n in range(2)]
        last_tanh = sem("last_tanh")
        last_gated = sem("last_gated")
        result_ready = sem("result_ready")
        out_done = [sem(f"out_done{n}") for n in range(2)]

        def alone(eng):
            eng.sem_inc(waited, 1)

        block = ctx.enter_context(nc.Block())
        before, first, mid, last, after = phases()

        def q_of(slot, h):
            return stack[:, slot, 0, h, :]

        def k_of(slot, h):
            return stack[:, slot, 1, h, :]

        def v_heads(v, c, n, h0=0, nh=HEADS):
            return v[:, c:c + n, h0 * VW:(h0 + nh) * VW].rearrange("p c (h e) -> p c h e", e=VW)

        def bank(ph, name, k):
            n = sum(ph.order[name, k])
            return turns[n % len(turns)] if ph.by_turns and name != "maxT" else aux

        def by_token(ap):
            return ap.rearrange("p (c e) -> p c e", c=2)

        def tokens(ap):
            return ap.rearrange("(n p) d -> p n d", p=P)

        @block.tensor
        def _(pe):
            mm = nc.tensor.matmul

            def max_scores(ph, i, h, kh):
                hp, kt = divmod(i, KT)
                slot = (hp + 2) % RING
                n = 32 * (GROUPS * ph.b + hp + 2) + 4 * kt + 2 * h + kh
                if (kt, h, kh) == (0, 0, 0):
                    pe.wait_ge(stack_in[slot], 16 * len(BLOCKS) * (2 * ph.b + (hp + 2) // RING + 1))
                wait_past(pe, scores_used, n - 1)
                mm(scores[kh][:, :], q_of(slot, h)[0:STACK, kt * P:(kt + 1) * P],
                   k_of(slot, h)[0:STACK, kh * HALF:(kh + 1) * HALF], start=True, stop=True).then_inc(scores_full, 1)

            def exponents(ph, i, h):
                hp, kt = divmod(i, KT)
                slot = hp % RING
                step = STEPS * ph.b + i
                if (kt, h) == (0, 0):
                    pe.wait_ge(max_loaded, 32 * (GROUPS * ph.b + hp + 1))
                wait_past(pe, exp_done, 2 * step - 1 + h)
                for qh in range(2):
                    one = mm(scoresT[h][:, qh, :], k_of(slot, h)[0:ROWS, kt * P:(kt + 1) * P],
                             q_of(slot, h)[0:ROWS, qh * HALF:(qh + 1) * HALF], start=True, stop=True)
                one.then_inc(scoresT_full, 1)

            def weigh_values(ph, i):
                step = STEPS * ph.b + i - 1
                hp, kt = divmod((i - 1) % STEPS, KT)
                pe.wait_ge(exp_done, 2 * step + 2)
                if kt == 0:
                    wait_past(pe, acc_used, GROUPS * ph.b + hp)
                    pe.wait_ge(v_in[chunk_of(hp)], 16 * (ph.b + 1))
                for h in range(2):
                    for qh in range(2):
                        j = 32 * (2 * h + qh)
                        head = 2 * hp + h
                        one = mm(acc[j:j + 32, :], v_now[:, kt, head * VW:head * VW + 32],
                                 probs[:, (i - 1) % 2, h, qh * HALF:(qh + 1) * HALF],
                                 start=(kt == 0), stop=(kt == KT - 1))
                one.then_inc(pv_done, 1)

            def project_features(dst, src, weight, et, th, more=None):
                pairs = [(s, u, dt) for s, u in [(src, weight)] + ([more] if more else []) for dt in range(DT)]
                for n, (s, u, dt) in enumerate(pairs):
                    one = mm(dst, w[:, u, dt, et * P:(et + 1) * P], s[:, dt, th * HALF:(th + 1) * HALF],
                             start=(n == 0), stop=(n == len(pairs) - 1))
                return one

            def project_tokens(dst, src, weight, k):
                for c in range(2):
                    for dt in range(DT):
                        t0 = (2 * k + c) * P
                        one = mm(by_token(dst)[:, c, :], src[:, dt, t0:t0 + P], w[:, weight, dt, :],
                                 start=(dt == 0), stop=(dt == DT - 1))
                return one

            def transpose_tokens(dst, src, k):
                th, dt = divmod(k, 2)
                for c in range(4):
                    one = nc.tensor.transpose(dst[:, c * P:(c + 1) * P], src[:, 4 * th + c, dt * P:(dt + 1) * P],
                                              ident[:, :])
                return one

            def wait_read(ph, name, k):
                pe.wait_ge(act_read if name in BY_ACT else dve_read, ph.read(name, k))

            def fill(ph, name, k):
                n = [(a, c) for _, a, c in ph.plan].index((name, k))
                by_turns = ph.by_turns
                back = len(turns) if by_turns and name != "maxT" else 1
                if n >= back:
                    wait_read(ph, *ph.plan[n - back][1:])
                elif n == 0:
                    wait_past(pe, act_read, ph.base[1])
                    wait_past(pe, dve_read, ph.base[0])
                dst = bank(ph, name, k)
                if name == "norm":
                    pe.wait_ge(acc_used, GROUPS * ph.b + k)
                    for c in range(4):
                        one = nc.tensor.transpose(dst[:, c * P:(c + 1) * P], o_raw[:, c * P:(c + 1) * P], ident[:, :])
                elif name == "maxT":
                    pe.wait_ge(max_split, GROUPS * ph.b + k + 2)
                    for qt in range(TT):
                        one = nc.tensor.transpose(dst.bitcast(BF16)[0:6, qt * P:(qt + 1) * P],
                                                  max_parts[:, qt, :, :].rearrange("p h a -> p (h a)"), ident_bf[:, :])
                elif name == "oT":
                    if by_turns:
                        wait_read(ph, "norm", 0)
                    one = transpose_tokens(dst, o_tok, k)
                elif name == "hT":
                    pe.wait_ge(ln_done[0], 2 * (ph.b + 1) + k // 2 + 1)
                    one = transpose_tokens(dst, xn, k)
                elif name == "h2T":
                    pe.wait_ge(ln_done[1], 2 * (ph.b - 1) + k // 2 + 1)
                    one = transpose_tokens(dst, xn, k)
                elif name == "qk":
                    if by_turns:
                        wait_read(ph, "hT", 2 * (k % 2) + 1)
                    one = project_features(dst, hT, WQ + k // 2 % 2, k // 4, k % 2)
                elif name == "v":
                    if by_turns:
                        wait_read(ph, "hT", 2 * (k // 2) + 1)
                    one = project_tokens(dst, hT, WV, k)
                elif name == "wo":
                    if by_turns:
                        wait_read(ph, "oT", 2 * (k // 2) + 1)
                    one = project_tokens(dst, fT, WO, k)
                elif name == "gate":
                    th, et, gate = k // 6, k // 3 % 2, k % 3
                    if by_turns:
                        wait_read(ph, "h2T", 2 * th + 1)
                    pe.wait_ge(cell_ready, 2 * ph.b)
                    one = project_features(dst, fT, WF + gate, et, th, (cell, UF + gate))
                elif name == "pre":
                    if by_turns:
                        wait_read(ph, "h2T", 2 * (k // 2) + 1)
                    one = project_tokens(dst, fT, WX, k)
                elif name == "fin":
                    pe.wait_ge(cell_ready, 2 * BATCH + k // 2 + 1)
                    one = project_tokens(dst, cell, UO, k)
                elif name == "modT":
                    for m in range(4):
                        for dt in range(DT):
                            for kt in range(DT):
                                c0 = MOD_COLS[m] * D + dt * P
                                o = (m * DT + dt) * BATCH
                                one = mm(dst[:, o:o + BATCH], wmod[:, kt, c0:c0 + P], silu[:, kt, :],
                                         start=(kt == 0), stop=(kt == DT - 1))
                elif name == "mod_rows":
                    for c in range(2):
                        for kt in range(DT):
                            col = (GA, GB)[k // 2] * D
                            one = mm(by_token(dst)[:, c, :], silu_wide[:, kt, 2 * (k % 2) + c, :],
                                     wmod[:, kt, col:col + D], start=(kt == 0), stop=(kt == DT - 1))
                one.then_inc(full, 1)

            def steps(ph, prior):
                for i in range(STEPS):
                    ahead = ph.qkv or i // KT < GROUPS - 2
                    exponents(ph, i, 0)
                    if ahead:
                        max_scores(ph, i, 0, 0)
                    exponents(ph, i, 1)
                    if ahead:
                        max_scores(ph, i, 0, 1)
                    if prior or i:
                        weigh_values(ph, i)
                    if ahead:
                        max_scores(ph, i, 1, 0)
                    if i in ph.at:
                        fill(ph, *ph.at[i])
                    if ahead:
                        max_scores(ph, i, 1, 1)

            pe.wait_ge(consts, 1)
            pe.wait_ge(silu_ready, 1)
            pe.wait_ge(mod_in, 32)
            for _, name, k in before.plan:
                if (name, k) == ("qk", 0):
                    pe.wait_ge(qkv_in, 80)
                if name == "maxT":
                    break
                fill(before, name, k)
            pe.wait_ge(act_read, before.end()[1] - 1)
            pe.wait_ge(dve_read, before.end()[0])
            for i in range(STEPS - 2 * KT, STEPS):
                for h in range(2):
                    for kh in range(2):
                        max_scores(before, i, h, kh)
                if i == STEPS - KT + 1:
                    fill(before, "maxT", GROUPS - 1)
            steps(first, False)
            pe.wait_ge(rest_in, 32)
            with pe.Fori(1, BATCH - 1) as b:
                steps(mid(b), True)
            steps(last, True)
            weigh_values(after, 0)
            pe.wait_ge(scores_used, 32 * GROUPS * BATCH)
            for _, name, k in after.plan:
                fill(after, name, k)

        @block.scalar
        def _(act):
            run = nc.scalar.activation

            def exponentials(ph, i):
                step = STEPS * ph.b + i
                wait_past(act, pv_done, step - 1)
                for h in range(2):
                    act.wait_ge(scoresT_full, 2 * step + h + 1)
                    run(probs[:, i % 2, h, :], scoresT[h].rearrange("p a b -> p (a b)"),
                        ACT.Exp).then_inc(exp_done, 1)

            def evacuate_output(ph, k):
                act.wait_ge(pv_done, STEPS * ph.b + KT * k)
                nc.scalar.copy(o_raw[:, :], acc[:, :]).then_inc(acc_used, 1)

            def evacuate(ph, name, k):
                if name not in BY_ACT:
                    return
                act.wait_ge(full, ph.full(name, k))
                src = bank(ph, name, k)
                th, dt = divmod(k, 2)
                half = slice(th * HALF, (th + 1) * HALF)
                if name == "maxT":
                    wait_past(act, max_loaded, 32 * (GROUPS * ph.b + k + 1))
                    nc.scalar.copy(max_rows[:, :], src.bitcast(BF16)[0:6, :]).then_inc(act_read, 1)
                elif name == "oT":
                    nc.scalar.copy(fT[:, dt, half], src).then_inc(act_read, 1)
                elif name == "hT":
                    nb = ph.b + 1
                    alone(act)
                    run(hT[:, dt, half], src, ACT.Identity, bias=modT[:, SA, dt, bass.ds(nb, 1)],
                        scale=modT[:, CA, dt, bass.ds(nb, 1)]).then_inc(act_read, 1)
                elif name == "h2T":
                    t = ph.b - 1
                    alone(act)
                    run(fT[:, dt, half], src, ACT.Identity, bias=modT[:, SB, dt, bass.ds(t, 1)],
                        scale=modT[:, CB, dt, bass.ds(t, 1)]).then_inc(act_read, 1)
                elif name == "qk":
                    n, which, et = k, k // 2 % 2, k // 4
                    wait_past(act, split_done, 8 * (ph.b + 1) + n - 1)
                    run(qk_f32[:, n % 2, :], src, ACT.Identity,
                        bias=cols[:, BQ + which, et:et + 1],
                        scale=1.0 if which else SCALE).then_inc(act_read, 1)
                elif name == "gate":
                    et, gate, n = k // 3 % 2, k % 3, k // 3
                    if gate == 0 and n >= 2:
                        act.wait_ge(gate_sum, 4 * (ph.b - 1) + n - 1)
                    run(gates[:, n % 2, gate, :], src, ACT.Tanh, bias=cols[:, BF + gate, et:et + 1],
                        scale=1.0 if gate == 2 else 0.5).then_inc(act_read, 1)

            def steps(ph, prior):
                for i in range(STEPS):
                    exponentials(ph, i)
                    if i % KT == 0 and (prior or i):
                        evacuate_output(ph, i // KT)
                    if i in ph.at:
                        evacuate(ph, *ph.at[i])

            act.wait_ge(mod_in, 32)
            run(cs_tanh[:, :, :], cs[:, :, :], ACT.Tanh, scale=0.5).then_inc(cs_tanhed, 1)
            act.wait_ge(mod_seq, 2)
            act.wait_ge(filled_once, 4)
            for _, name, k in before.plan:
                evacuate(before, name, k)
            steps(first, False)
            with act.Fori(1, BATCH - 1) as b:
                steps(mid(b), True)
            steps(last, True)
            evacuate_output(after, 0)
            for _, name, k in after.plan:
                evacuate(after, name, k)
                if name == "fin":
                    act.wait_ge(dve_read, after.read("fin", k))
                    r = result[k % 2]
                    run(r[:, :, :, :], r[:, :, :, :], ACT.Tanh).then_inc(last_tanh, 1)

        @block.vector
        def _(dve):
            v = nc.vector

            def maximum(ph, i, h, kh):
                hp, kt = divmod(i, KT)
                n = 32 * (GROUPS * ph.b + hp + 2) + 4 * kt + 2 * h + kh
                dve.wait_ge(scores_full, n + 1)
                col = (2 * kt + h) * 2 + kh
                v.tensor_reduce(max_half[:, hp % 2, col:col + 1], scores[kh][:, :], AX.X,
                                ALU.max).then_inc(scores_used, 1)

            def split_maxima(ph, hp, stage):
                g = GROUPS * ph.b + hp + 1
                if stage == 0:
                    dve.wait_ge(scores_used, 32 * (g + 1))
                    v.tensor_reduce(neg_max[:, :, :], max_half[:, (hp + 1) % 2, :].rearrange(
                        "p (q h k) -> p q h k", h=2, k=2), AX.X, ALU.max, negate=True).then_inc(max_seq, 1)
                elif stage == 1:
                    dve.wait_ge(max_seq, 4 * g + 1)
                    wait_past(dve, max_loaded, 32 * g)
                    v.tensor_copy(max_parts[:, :, :, 0], neg_max[:, :, :]).then_inc(max_seq, 1)
                    dve.wait_ge(max_seq, 4 * g + 2)
                    v.tensor_tensor(max_rest[:, :, :], neg_max[:, :, :], max_parts[:, :, :, 0],
                                    ALU.subtract).then_inc(max_seq, 1)
                else:
                    dve.wait_ge(max_seq, 4 * g + 3)
                    v.tensor_copy(max_parts[:, :, :, 1], max_rest[:, :, :]).then_inc(max_seq, 1)
                    dve.wait_ge(max_seq, 4 * g + 4)
                    v.tensor_tensor(max_parts[:, :, :, 2], max_rest[:, :, :], max_parts[:, :, :, 1],
                                    ALU.subtract).then_inc(max_split, 1)

            def norm_stats(which, src, tiles):
                for n in tiles:
                    one = v.bn_stats(stats[:, which, n, :], src[:, n, :])
                if tiles[-1] % 4 == 3:
                    one.then_inc(stats_ready[which], 1)

            def norm_moments(which, n, th):
                dve.wait_ge(stats_ready[which], 2 * n + th + 1)
                alone(dve)
                for t in range(4 * th, 4 * th + 4):
                    one = v.bn_aggr(mean_var[:, which, t, :], stats[:, which, t, :])
                one.then_inc(mean_ready[which], 1)
                dve.wait_ge(mean_ready[which], 2 * n + th + 1)
                v.tensor_scalar(var_eps[:, which, 4 * th:4 * th + 4], mean_var[:, which, 4 * th:4 * th + 4, 1], EPS,
                                None, ALU.add).then_inc(var_ready[which], 1)

            def norm_apply(which, n, src, th):
                dve.wait_ge(rstd_ready[which], 2 * n + th + 1)
                for t in range(4 * th, 4 * th + 4):
                    one = v.tensor_scalar(xn[:, t, :], src[:, t, :], mean_var[:, which, t, 0:1],
                                          rstd[:, which, t:t + 1], ALU.subtract, ALU.mult)
                one.then_inc(ln_done[which], 1)

            def split(ph, k):
                dve.wait_ge(act_read, ph.read("qk", k))
                wait_past(dve, parts_out[k % 2], 16 * (k // 2))
                whole = qk_f32[:, k % 2, :]
                part = [parts[:, k % 2, c, :] for c in range(3)]
                v.tensor_copy(part[0], whole).then_inc(split_seq, 1)
                dve.wait_ge(split_seq, 3 * k + 1)
                v.tensor_tensor(rest[:, :], whole, part[0], ALU.subtract).then_inc(split_seq, 1)
                dve.wait_ge(split_seq, 3 * k + 2)
                v.tensor_copy(part[1], rest[:, :]).then_inc(split_seq, 1)
                dve.wait_ge(split_seq, 3 * k + 3)
                v.tensor_tensor(part[2], rest[:, :], part[1], ALU.subtract).then_inc(split_done, 1)

            def sum_gates(ph, n):
                th, et = divmod(n, 2)
                half = slice(th * HALF, (th + 1) * HALF)
                f, i, g = (gates[:, n % 2, m, :] for m in range(GATES))
                m = 4 * (ph.b - 1) + n
                dve.wait_ge(act_read, ph.read("gate", 3 * n + 2))
                dve.wait_ge(cell_ready, 2 * ph.b + th)
                v.scalar_tensor_tensor(f, f, 1.0, cell[:, et, half], ALU.add, ALU.mult).then_inc(gate_seq, 1)
                v.scalar_tensor_tensor(i, i, 1.0, g, ALU.add, ALU.mult).then_inc(gate_seq, 1)
                dve.wait_ge(gate_seq, 2 * m + 2)
                v.tensor_tensor(cell_sum[:, et, :], f, i, ALU.add).then_inc(gate_sum, 1)

            def evacuate(ph, name, k):
                if name not in ("norm", "v", "wo", "pre"):
                    return
                dve.wait_ge(full, ph.full(name, k))
                src = bank(ph, name, k)
                if name == "norm":
                    hp = (k - 1) % GROUPS
                    o = src.rearrange("p (c j e) -> p c j e", c=4, j=4)
                    v.reciprocal(inv_sum[:, :, :], o[:, :, :, DK]).then_inc(sums_inverted, 1)
                    dve.wait_ge(sums_inverted, GROUPS * ph.b + k)
                    for h in range(2):
                        head = 2 * hp + h
                        one = v.tensor_tensor(
                            o_tok.rearrange("p (q c) d -> p q c d", q=2)[:, :, :, head * DK:(head + 1) * DK],
                            o.rearrange("p c j e -> p j c e")[:, 2 * h:2 * h + 2, :, 0:DK],
                            inv_sum.rearrange("p c j -> p j c")[:, 2 * h:2 * h + 2, :].unsqueeze(3).to_broadcast(
                                [P, 2, 4, DK]), ALU.mult)
                    one.then_inc(dve_read, 1)
                elif name == "v":
                    wait_past(dve, v_in[-1], 16 * (ph.b + 1))
                    bias = rows[:, BV, :].rearrange("p (h d) -> p h d", d=DK).unsqueeze(1).to_broadcast(
                        [P, 2, HEADS, DK])
                    one = v.tensor_tensor(v_heads(v_next, 2 * k, 2)[:, :, :, 0:DK],
                                          src.rearrange("p (c h d) -> p c h d", c=2, d=DK), bias, ALU.add)
                    if k == 0:
                        one.then_inc(v_added, 1)
                        dve.wait_ge(v_added, ph.b + 2)
                        first_key = v_heads(v_next, 0, 1)[0:1, 0, :, 0:DK]
                        one = v.tensor_scalar(first_key, first_key, 0.5, None, ALU.mult)
                    one.then_inc(dve_read, 1)
                elif name == "wo":
                    t = ph.b - 1
                    if k >= 2:
                        dve.wait_ge(x1_ready, 4 * t + k - 1)
                    v.tensor_tensor(attn[:, k % 2, :, :], by_token(src), mod_rows[:, 0, bass.ds(t, 1), :].to_broadcast(
                        [P, 2, D]), ALU.mult).then_inc(dve_read, 1)
                elif name == "pre":
                    t = ph.b - 1
                    if k >= 2 and not ph.by_turns:
                        dve.wait_ge(pre_out[k % 2], 16 * (2 * t + 1))
                    dst = pre[:, k % 2, :, :] if not ph.by_turns else pre_all[:, t, 2 * k:2 * k + 2, :]
                    v.tensor_tensor(dst, by_token(src), rows[:, BH:BH + 1, :].to_broadcast(
                        [P, 2, D]), ALU.add).then_inc(dve_read, 1)

            def stats_after_attention(ph, k):
                dve.wait_ge(x1_ready, 4 * (ph.b - 1) + k + 1)
                norm_stats(1, x1, [2 * k, 2 * k + 1])

            def add_last(k):
                if k == 0:
                    dve.wait_ge(pre_in, 16 * (BATCH - 1))
                if k >= 2:
                    dve.wait_ge(out_done[k % 2], 16 * BATCH)
                dve.wait_ge(dve_read, after.read("pre", k))
                dve.wait_ge(full, after.full("fin", k))
                v.tensor_tensor(result[k % 2].rearrange("p t n d -> p t (n d)"),
                                bank(after, "fin", k).unsqueeze(1).to_broadcast([P, BATCH, HALF]),
                                pre_all[:, :, 2 * k:2 * k + 2, :].rearrange("p t n d -> p t (n d)"),
                                ALU.add).then_inc(dve_read, 1)

            def gate_last(k):
                dve.wait_ge(last_tanh, k + 1)
                r = result[k % 2]
                gb = mod_rows[:, 1, :, :].unsqueeze(2).to_broadcast([P, BATCH, 2, D])
                v.tensor_tensor(r[:, :, :, :], r[:, :, :, :], gb, ALU.mult).then_inc(last_gated, 1)

            def steps(ph):
                for i in range(STEPS):
                    hp, kt = divmod(i, KT)
                    if kt < 3 and (ph.qkv or hp < GROUPS - 1):
                        split_maxima(ph, hp, kt)
                    if ph.qkv or hp < GROUPS - 2:
                        for h in range(2):
                            for kh in range(2):
                                maximum(ph, i, h, kh)
                    if i in ph.at:
                        evacuate(ph, *ph.at[i])
                    if ph.qkv and i == 4:
                        dve.wait_ge(xn_in, 16 * (ph.b + 2))
                    if ph.qkv and 4 <= i < 8:
                        norm_stats(0, xn, [2 * (i - 4), 2 * (i - 4) + 1])
                    if ph.qkv and i in (8, 9):
                        norm_moments(0, ph.b + 1, i - 8)
                    if ph.qkv and i in (10, 11):
                        norm_apply(0, ph.b + 1, xn, i - 10)
                    if ph.post and 14 <= i < 18:
                        stats_after_attention(ph, i - 14)
                    if ph.post and i in (18, 19):
                        norm_moments(1, ph.b - 1, i - 18)
                    if ph.post and i in (20, 21):
                        if ph.qkv:
                            dve.wait_ge(act_read, ph.read("hT", 3))
                        norm_apply(1, ph.b - 1, x1, i - 20)
                    name, k = ph.at.get(i - 1, (None, 0))
                    if name == "gate" and k % 3 == 2:
                        sum_gates(ph, k // 3)

            v.memset(v_next[:, :, :], 1.0)
            v.memset(v_now[:, :, :], 1.0)
            v.memset(stack[STACK:ROWS, :, 1, :, :], 1.0).then_inc(filled_once, 1)
            dve.wait_ge(mod_in, 32)
            dve.wait_ge(cs_tanhed, 1)
            v.scalar_tensor_tensor(silu[:, :, :], cs_tanh[:, :, :], 1.0, cs[:, :, :], ALU.add,
                                   ALU.mult).then_inc(filled_once, 1)
            dve.wait_ge(filled_once, 2)
            v.tensor_scalar(silu[:, :, :], silu[:, :, :], 0.5, None, ALU.mult).then_inc(filled_once, 1)
            dve.wait_ge(filled_once, 3)
            v.tensor_copy(silu_wide[:, :, :, :], silu[:, :, :].unsqueeze(3).to_broadcast(
                [P, DT, BATCH, P])).then_inc(silu_ready, 1)
            dve.wait_ge(xn_in, 16)
            for th in range(2):
                norm_stats(0, xn, list(range(4 * th, 4 * th + 4)))
                norm_moments(0, 0, th)
            dve.wait_ge(qkv_in, 80)
            v.tensor_scalar(cols[:, BQ, :], cols[:, BQ, :], SCALE, None, ALU.mult)
            v.tensor_scalar(cols[:, BF:BI + 1, :], cols[:, BF:BI + 1, :], 0.5, None, ALU.mult).then_inc(filled_once, 1)
            for th in range(2):
                norm_apply(0, 0, xn, th)
            dve.wait_ge(full, before.full("modT", 0))
            v.tensor_copy(modT.rearrange("p m t b -> p (m t b)"),
                          bank(before, "modT", 0)[:, 0:4 * DT * BATCH]).then_inc(dve_read, 1)
            dve.wait_ge(dve_read, before.read("modT", 0))
            v.tensor_scalar(modT[:, CA, :, :], modT[:, CA, :, :], 1.0, None, ALU.add).then_inc(mod_seq, 1)
            v.tensor_scalar(modT[:, CB, :, :], modT[:, CB, :, :], 1.0, None, ALU.add).then_inc(mod_seq, 1)
            for _, name, k in before.plan:
                if name == "v":
                    evacuate(before, "v", k)
                if name == "qk":
                    split(before, k)
            for k in range(4):
                dve.wait_ge(full, before.full("mod_rows", k))
                b0 = 2 * (k % 2)
                v.tensor_copy(mod_rows[:, k // 2, b0:b0 + 2, :],
                              by_token(bank(before, "mod_rows", k))).then_inc(dve_read, 1)
            dve.wait_ge(dve_read, before.read("mod_rows", 3))
            v.tensor_scalar(mod_sign[:, :, :, :], mod_rows[:, :, :, :], 0.0, 2.0, ALU.is_ge, ALU.mult).then_inc(mod_seq, 1)
            dve.wait_ge(mod_seq, 3)
            v.tensor_scalar(mod_sign[:, :, :, :], mod_sign[:, :, :, :], -1.0, None, ALU.add).then_inc(mod_seq, 1)
            dve.wait_ge(mod_seq, 4)
            v.tensor_tensor(mod_rows[:, :, :, :], mod_rows[:, :, :, :], mod_sign[:, :, :, :], ALU.mult).then_inc(mod_seq, 1)
            dve.wait_ge(mod_seq, 5)
            v.scalar_tensor_tensor(mod_rows.rearrange("p a b d -> p (a b d)"), mod_rows.rearrange("p a b d -> p (a b d)"),
                                   0.25, mod_sign.rearrange("p a b d -> p (a b d)"), ALU.max,
                                   ALU.mult).then_inc(mod_seq, 1)
            dve.wait_ge(mod_seq, 6)
            v.tensor_tensor(ga_bo, mod_rows[:, 0, :, :], rows[:, BO:BO + 1, :].to_broadcast([P, BATCH, D]),
                            ALU.mult).then_inc(mod_ready, 1)
            for et in range(DT):
                v.tensor_copy(cell[:, et, :], cols[:, C0, et:et + 1].to_broadcast([P, L])).then_inc(cell_ready, 1)
            for i in range(STEPS - 2 * KT, STEPS):
                hp, kt = divmod(i, KT)
                if hp == GROUPS - 1 and kt == 0:
                    for stage in range(3):
                        split_maxima(before, hp, stage)
                for h in range(2):
                    for kh in range(2):
                        maximum(before, i, h, kh)
            steps(first)
            with dve.Fori(1, BATCH - 1) as b:
                steps(mid(b))
            steps(last)
            for _, name, k in after.plan:
                if name == "fin":
                    add_last(k)
                    continue
                evacuate(after, name, k)
                if name == "wo":
                    stats_after_attention(after, k)
                    if k % 2:
                        norm_moments(1, BATCH - 1, k // 2)
                        norm_apply(1, BATCH - 1, x1, k // 2)
                if name == "gate" and k % 3 == 2:
                    sum_gates(after, k // 3)
                if (name, k) == ("gate", 11):
                    for chunk in range(2):
                        gate_last(chunk)
            for chunk in range(2, 4):
                gate_last(chunk)

        @block.gpsimd
        def _(pool):
            g = nc.gpsimd

            def split(ph, k):
                n, m = k, 8 * (ph.b + 1) + k
                pool.wait_ge(act_read, ph.read("qk", k))
                wait_past(pool, parts_out[n % 2], 16 * (4 * (ph.b + 1) + n // 2))
                alone(pool)
                whole = qk_f32[:, n % 2, :]
                part = [parts[:, n % 2, c, :] for c in range(3)]
                g.tensor_scalar(part[0], whole, 1.0, 0.0, ALU.mult, ALU.add).then_inc(split_seq, 1)
                pool.wait_ge(split_seq, 3 * m + 1)
                g.tensor_tensor(rest[:, :], whole, part[0], ALU.subtract).then_inc(split_seq, 1)
                pool.wait_ge(split_seq, 3 * m + 2)
                alone(pool)
                g.tensor_scalar(part[1], rest[:, :], 1.0, 0.0, ALU.mult, ALU.add).then_inc(split_seq, 1)
                pool.wait_ge(split_seq, 3 * m + 3)
                g.tensor_tensor(part[2], rest[:, :], part[1], ALU.subtract).then_inc(split_done, 1)

            def inverse_deviation(which, n, th):
                pool.wait_ge(var_ready[which], 2 * n + th + 1)
                four = slice(4 * th, 4 * th + 4)
                g.tensor_tensor(rstd[:, which, four], var_eps[:, which, four], minus_half[:, four],
                                ALU.pow).then_inc(rstd_ready[which], 1)

            def bias_residual(ph):
                t = ph.b - 1
                pool.wait_ge(res_in, 16 * ph.b)
                g.tensor_tensor(x1[:, :, :], x1[:, :, :], ga_bo[:, bass.ds(t, 1), :].to_broadcast([P, TT, D]),
                                ALU.add).then_inc(res_biased, 1)

            def add_residual(ph, k):
                pool.wait_ge(dve_read, ph.read("wo", k))
                pool.wait_ge(res_biased, ph.b)
                two = x1[:, 2 * k:2 * k + 2, :]
                g.tensor_tensor(two, attn[:, k % 2, :, :], two, ALU.add).then_inc(x1_ready, 1)

            def halve_cell(ph, th):
                pool.wait_ge(gate_sum, 4 * (ph.b - 1) + 2 * th + 2)
                alone(pool)
                g.tensor_scalar(cell[:, :, th * HALF:(th + 1) * HALF], cell_sum[:, :, :], 0.5, 0.0, ALU.mult,
                                ALU.add).then_inc(cell_ready, 1)

            def steps(ph):
                for i in range(STEPS):
                    name, k = ph.at.get(i, (None, 0))
                    if ph.post and i == 1:
                        bias_residual(ph)
                    if name == "qk":
                        split(ph, k)
                    if name == "wo":
                        add_residual(ph, k)
                    if ph.qkv and i in (8, 9):
                        inverse_deviation(0, ph.b + 1, i - 8)
                    if ph.post and i in (18, 19):
                        inverse_deviation(1, ph.b - 1, i - 18)
                    name, k = ph.at.get(i - 1, (None, 0))
                    if name == "gate" and k % 6 == 5:
                        halve_cell(ph, k // 6)

            g.memset(ident[:, :], 0.0)
            g.memset(ident_bf[:, :], 0.0)
            g.memset(minus_half[:, :], -0.5).then_inc(zeros, 1)
            pool.wait_ge(zeros, 1)
            g.affine_select(out=ident[:, :], in_=ident[:, :], compare_op=ALU.not_equal, fill=1.0, base=0,
                            pattern=[[-1, P]], channel_multiplier=1)
            g.affine_select(out=ident_bf[:, :], in_=ident_bf[:, :], compare_op=ALU.not_equal, fill=1.0, base=0,
                            pattern=[[-1, P]], channel_multiplier=1).then_inc(consts, 1)
            for th in range(2):
                inverse_deviation(0, 0, th)
            pool.wait_ge(mod_ready, 1)
            steps(first)
            with pool.Fori(1, BATCH - 1) as b:
                steps(mid(b))
            steps(last)
            bias_residual(after)
            for _, name, k in after.plan:
                if name == "wo":
                    add_residual(after, k)
                if name == "wo" and k % 2:
                    inverse_deviation(1, BATCH - 1, k // 2)
                if name == "gate" and k % 6 == 5:
                    halve_cell(after, k // 6)
            for k in range(4):
                pool.wait_ge(last_gated, k + 1)
                pool.wait_ge(x1_in[k % 2], 16 * (BATCH - 1) * (k // 2 + 1))
                r = result[k % 2]
                z = BATCH - 1
                g.tensor_tensor(r[:, z, :, :], r[:, z, :, :], x1[:, 2 * k:2 * k + 2, :], ALU.add)
                g.tensor_tensor(r[:, 0:z, :, :], r[:, 0:z, :, :], x1_chunk[:, k % 2, 0:z], ALU.add).then_inc(result_ready, 1)

        @block.sync
        def _(sp):
            def load_stack(ph, hp):
                nb, h3 = (ph.b, hp + 3) if hp + 3 < GROUPS else (ph.b + 1, hp + 3 - GROUPS)
                slot = (hp + 3) % RING
                if h3 in (0, GROUPS // 2):
                    for n in range(2):
                        sp.wait_ge(parts_out[n], 64 * nb + (32 if h3 == 0 else 64))
                        alone(sp)
                wait_past(sp, scoresT_full, 2 * KT * (GROUPS * ph.b + hp))
                alone(sp)
                part_of = pieces[bass.ds(nb, 1)].rearrange("o k c (g h d) t -> (o k) c g h d t", g=GROUPS, h=2)
                for block, qk, part in BLOCKS:
                    r = block * DK
                    sp.dma_start(stack[r:r + DK, slot, qk, :, :], part_of[qk, part, h3].rearrange(
                        "h d t -> d h t")).then_inc(stack_in[slot], 16)

            def move_values(c, batch, groups_done):
                lo, hi = V_CHUNKS[c]
                wait_past(sp, pv_done, KT * groups_done)
                a, z = 2 * lo * VW, 2 * (hi + 1) * VW
                sp.dma_start(v_now[:, :, a:z], v_next[:, :, a:z]).then_inc(v_in[c], 16)

            def place_maxima(ph, hp):
                slot = (hp + 1) % RING
                sp.wait_ge(act_read, ph.read("maxT", hp))
                for h in range(2):
                    sp.dma_start(stack[STACK:ROWS, slot, 0, h, :], max_rows[3 * h:3 * h + 3, :]).then_inc(max_loaded, 16)

            def store_parts(ph, k):
                et, which, th = k // 4, k // 2 % 2, k % 2
                sp.wait_ge(split_done, 8 * (ph.b + 1) + k + 1)
                alone(sp)
                dst = pieces[bass.ds(ph.b + 1, 1), which, :, et * P:(et + 1) * P, th * HALF:(th + 1) * HALF]
                sp.dma_start(dst.rearrange("o c p t -> p (o c) t"), parts[:, k % 2, :, :]).then_inc(parts_out[k % 2], 16)

            def load_residual(ph):
                sp.wait_ge(act_read, ph.base[1])
                alone(sp)
                sp.dma_start(x1[:, :, :], tokens(x[bass.ds(ph.b - 1, 1)].rearrange("o n d -> (o n) d"))).then_inc(res_in, 16)

            def store_pre(ph, k):
                t = ph.b - 1
                sp.wait_ge(dve_read, ph.read("pre", k))
                alone(sp)
                sp.dma_start(pre_spill[:, bass.ds(t, 1), 2 * k:2 * k + 2, :].rearrange("p o n d -> p (o n) d"),
                             pre[:, k % 2, :, :]).then_inc(pre_out[k % 2], 16)

            def store_x1(ph):
                sp.wait_ge(x1_ready, 4 * ph.b)
                alone(sp)
                sp.dma_start(x1_spill[:, bass.ds(ph.b - 1, 1), :, :].rearrange("p o n d -> p (o n) d"),
                             x1[:, :, :]).then_inc(x1_out, 16)

            def store_result(k):
                sp.wait_ge(result_ready, k + 1)
                for t in range(BATCH):
                    sp.dma_start(tokens(out[t])[:, 2 * k:2 * k + 2, :], result[k % 2][:, t]).then_inc(out_done[k % 2], 16)

            def spilled(ph):
                sp.wait_ge(x1_out, 16 * ph.b)
                alone(sp)
                for n in range(2):
                    sp.wait_ge(pre_out[n], 32 * ph.b)
                    alone(sp)

            def steps(ph):
                for i in range(STEPS):
                    hp, kt = divmod(i, KT)
                    if kt == 4 and (ph.qkv or hp < GROUPS - 1):
                        place_maxima(ph, hp)
                    if i == 0 and ph.qkv:
                        sp.wait_ge(act_read, ph.base[1])
                        alone(sp)
                        sp.dma_start(xn[:, :, :], tokens(x[bass.ds(ph.b + 1, 1)].rearrange("o n d -> (o n) d"))
                                     ).then_inc(xn_in, 16)
                    if i == 0 and ph.post:
                        load_residual(ph)
                    if kt == 0 and (ph.qkv or hp + 3 < GROUPS):
                        load_stack(ph, hp)
                    if i == 1:
                        move_values(3, ph.b, GROUPS * ph.b)
                    if kt == 1 and hp >= 5 and ph.qkv:
                        move_values(hp - 5, ph.b + 1, GROUPS * ph.b + V_CHUNKS[hp - 5][1] + 1)
                    name, k = ph.at.get(i - 1, (None, 0))
                    if name == "qk":
                        store_parts(ph, k)
                    if name == "pre":
                        store_pre(ph, k)
                    if ph.post and i == 18:
                        store_x1(ph)
                    if ph.post and i == STEPS - 1:
                        spilled(ph)

            sp.dma_start(cs[:, :, :], cT.rearrange("(t p) b -> p t b", p=P)).then_inc(mod_in, 16)
            sp.dma_start(xn[:, :, :], tokens(x[0])).then_inc(xn_in, 16)
            sp.dma_start(wmod, wmod_in.rearrange("(t p) n -> p t n", p=P)).then_inc(mod_in, 16)
            sp.dma_start(cols[:, :, :], cols_in).then_inc(qkv_in, 16)
            for n in range(3):
                sp.dma_start(rows[:, n, :], rows_in[n].partition_broadcast(P)).then_inc(qkv_in, 16)
            sp.dma_start(w[:, WQ:WV + 1, :, :], w_all[:, WQ:WV + 1, :, :]).then_inc(qkv_in, 16)
            sp.dma_start(w[:, WO:WX + 1, :, :], w_all[:, WO:WX + 1, :, :]).then_inc(rest_in, 16)
            sp.dma_start(w[:, UF:UO + 1, :, :], w_all[:, UF:UO + 1, :, :]).then_inc(rest_in, 16)
            sp.wait_ge(filled_once, 1)
            for k in range(8):
                store_parts(before, k)
                if k == 3:
                    for hp in (5, 6, 7):
                        load_stack(before, hp)
                    sp.wait_ge(dve_read, before.read("v", 3))
                    for c in range(3):
                        move_values(c, 0, 0)
            place_maxima(before, GROUPS - 1)
            steps(first)
            with sp.Fori(1, BATCH - 1) as b:
                steps(mid(b))
            steps(last)
            load_residual(after)
            sp.wait_ge(scoresT_full, 2 * STEPS * BATCH)
            for t in range(BATCH - 1):
                sp.dma_start(pre_all[:, t], pre_spill[:, t]).then_inc(pre_in, 16)

            def load_x1(k):
                for t in range(BATCH - 1):
                    sp.dma_start(x1_chunk[:, k % 2, t], x1_spill[:, t, 2 * k:2 * k + 2, :]).then_inc(x1_in[k % 2], 16)

            sp.wait_ge(pv_done, STEPS * BATCH)
            load_x1(0)
            load_x1(1)
            for k in range(4):
                store_result(k)
                if k < 2:
                    load_x1(k + 2)
            for n in range(2):
                sp.wait_ge(out_done[n], 16 * 2 * BATCH)

    return nc


def kernel(**inputs):
    import numpy as np
    import concourse.bacc as bacc
    from concourse.bass_utils import run_bass_kernel_spmd as run

    a = {name: np.asarray(v) for name, v in inputs.items()}
    matrices = [a[f"L0_attn_W{n}"] for n in "qkvo"] + [a[f"L0_ffn_{n}"] for n in
                                                      ("wf", "wi", "wc", "wo", "uf", "ui", "uc", "uo")]
    columns = [a["L0_attn_bq"], a["L0_attn_bk"], a["L0_ffn_bf"], a["L0_ffn_bi"], a["L0_ffn_bc"], a["L0_ffn_in_c"]]
    arrays = {
        "x": a["L0_attn_x"],
        "w_all": np.stack(matrices).transpose(2, 0, 1).reshape(DT, P, 12, D).transpose(1, 2, 0, 3),
        "cols": np.stack(columns).reshape(6, DT, P).transpose(2, 0, 1),
        "rows": np.stack([a["L0_attn_bv"], a["L0_attn_bo"], a["L0_ffn_bo"]]),
        "cT": a["L0_c"].T,
        "wmod": a["L0_wmod"],
    }
    arrays = {n: np.ascontiguousarray(v) for n, v in arrays.items()}
    nc = bacc.Bacc("TRN2", target_bir_lowering=False, num_devices=1)
    args = [nc.dram_tensor(f"in_{n}", v.shape, mybir.dt.from_np(v.dtype), kind="ExternalInput").ap() for n, v in arrays.items()]
    args += [nc.dram_tensor("pieces", (BATCH, 2, 3, D, L), BF16, kind="Internal").ap(),
             nc.dram_tensor("x1_spill", (P, BATCH, TT, D), F32, kind="Internal").ap(),
             nc.dram_tensor("pre_spill", (P, BATCH, TT, D), F32, kind="Internal").ap()]
    args.append(nc.dram_tensor("y", (BATCH, L, D), F32, kind="ExternalOutput").ap())
    adaln_layer(nc, *args)
    r = run(nc, [{f"in_{n}": v for n, v in arrays.items()}], core_ids=[0])
    return r.results[0]["y"]
```

```python
from contextlib import ExitStack

import concourse.bass as bass
from concourse import mybir

F32 = mybir.dt.float32
BF16 = mybir.dt.bfloat16
F32R = mybir.dt.float32r
ALU = mybir.AluOpType
ACT = mybir.ActivationFunctionType
AX = mybir.AxisListType

P = 128
BATCH, L, D = 4, 1024, 256
HEADS = 16
DK = D // HEADS
DT = D // P
TT = L // P
HALF = L // 2
GROUPS = HEADS // 2
KT = L // P
STEPS = GROUPS * KT
BANKS = 3
RING = 4
STACK = 6 * DK
ROWS = STACK + 3
VW = DK + 1
VPITCH = HEADS * VW + 16
SCALE = DK ** -0.5
EPS = 1e-5
GATES = 3
GATE_RING = 4

WQ, WK, WV, WO, WF, WI, WC, WX, UF, UI, UC = range(11)
BQ, BK, BF, BI, BC, C0 = range(6)
BV, BO, BH = range(3)
SA, CA, SB, CB = range(4)
MOD_COLS = (0, 1, 3, 4)
GA, GB = 2, 5

PRODUCTS = ((0, 0), (0, 1), (0, 2), (1, 0), (1, 1), (2, 0))
BLOCKS = [(n, qk, product[qk]) for n, product in enumerate(PRODUCTS) for qk in range(2)]

NORM2_STATS = range(20, 24)
NORM2_MOMENTS = range(24, 26)
NORM2_APPLY = range(28, 32)
NORM1_APPLY = range(12, 16)


def pair_of_tiles(i, steps):
    k = steps.index(i)
    return [2 * k, 2 * k + 1]


V_CHUNKS = ((0, 4), (5, 5), (6, 6), (7, 7))


def chunk_of(hp):
    return max(0, hp - 4)


FEATURES = ("oT", "hT", "h2T")
BY_ACT = ("maxT", "oT", "hT", "h2T", "qk", "gate", "mod_rows")


class Phase:

    QKV = [("hT", range(4)), ("qk", range(8)), ("v", range(4))]
    POST = [("oT", range(4)), ("wo", range(4))]
    FFN = [("h2T", range(4)), ("gate", range(6)), ("pre", range(4)), ("gate", range(6, 12))]

    def __init__(self, b, base, split_base, qkv, post, plan=None):
        self.b, self.base, self.split_base, self.qkv, self.post = b, base, split_base, qkv, post
        self.by_turns = plan is not None
        self.plan = self.of_steps() if plan is None else plan
        self.order, n = {}, [0, 0]
        for _, name, k in self.plan:
            self.order[name, k] = tuple(n)
            n[name in BY_ACT] += 1
        self.size = tuple(n)
        late = [(name, k) for i, name, k in self.plan if i is not None and not maxima_run(self, i)]
        self.beside = late[1::2]
        self.late = late
        self.features = [(name, k) for _, name, k in self.plan if name in FEATURES]
        self.at = {step: (name, k) for step, name, k in self.plan}

    def of_steps(self):
        free = [i for i in range(STEPS) if i % KT not in (2, 3)]
        dense = [(n, k) for n, ks in self.POST + self.QKV + self.FFN for k in ks]
        of_next = [n for n, _ in self.QKV]
        plan = []
        for i, (name, k) in zip(free[2:], dense):
            if self.qkv if name in of_next else self.post:
                plan.append((i, name, k))
        for hp in range(GROUPS):
            if self.post or hp:
                plan.append((hp * KT + 2, "norm", hp))
            if self.qkv or hp < GROUPS - 1:
                plan.append((hp * KT + 3, "maxT", hp))
        return sorted(plan)

    def full(self, name, k):
        return sum(self.base) + sum(self.order[name, k]) + 1

    def read(self, name, k):
        who = name in BY_ACT
        return self.base[who] + self.order[name, k][who] + 1

    def split(self, name, k):
        return self.split_base + self.features.index((name, k)) + 1

    def end(self):
        return self.base[0] + self.size[0], self.base[1] + self.size[1]


def planned(*parts):
    return [(None, name, k) for name, ks in parts for k in ks]


PROLOGUE = planned(("modT", [0]), ("hT", range(4)), ("qk", range(4)), ("v", range(4)), ("modT", [1]),
                   ("mod_rows", range(4)), ("qk", range(4, 8)), ("maxT", [GROUPS - 1]))
TAIL = planned(("norm", [0]), ("oT", range(4)), ("wo", range(4)), ("h2T", [0, 1]), ("gate", range(3)),
               ("h2T", [2, 3]), ("gate", range(3, 6)), ("pre", [0, 1]), ("gate", range(6, 9)), ("fin", [0, 1]),
               ("gate", range(9, 12)), ("pre", [2, 3]), ("fin", [2, 3]))


def phases():
    before = Phase(-1, (0, 0), 0, True, False, PROLOGUE)
    first = Phase(0, before.end(), 4, True, False)
    start, one = first.end(), Phase(1, (0, 0), 0, True, True)

    def between(b):
        n = b - 1
        return (start[0] + n * one.size[0], start[1] + n * one.size[1]), 8 + n * len(one.features)

    def mid(b):
        return Phase(b, *between(b), True, True)

    last = Phase(BATCH - 1, *between(BATCH - 1), False, True)
    after = Phase(BATCH, last.end(), last.split_base + len(last.features), False, True, TAIL)
    return before, first, mid, last, after


def freed(m, n):
    before = 4 * STEPS - 1
    return n - (BANKS if m >= BANKS else m + 1 + (before - m % BANKS) % BANKS) + 1


def maxima_run(ph, i):
    return ph.qkv or i < STEPS - 2 * KT


def wait_past(eng, sem, value):
    if not isinstance(value, int) or value > 0:
        eng.wait_ge(sem, value)


def adaln_layer(nc, x, w_all, cols_in, rows_in, cT, wmod_in, pieces, x1_spill, pre_spill, out):
    ctx = ExitStack()
    with ctx:
        def sb(name, shape, dt=F32):
            return ctx.enter_context(nc.sbuf_tensor(name, shape, dt))[:]

        def pb(name, shape, dt=F32):
            return ctx.enter_context(nc.psum_tensor(name, shape, dt))[:]

        def sem(name):
            return ctx.enter_context(nc.semaphore(name))

        stack = sb("stack", [P, RING, 2, 2, L], BF16)
        probs = sb("probs", [P, 2, 2, L])
        v_now = sb("v_now", [P, KT, VPITCH])
        v_next = sb("v_next", [P, KT, VPITCH])
        w_hi = sb("w_hi", [P, 11, DT, D], F32R)
        w_lo = sb("w_lo", [P, 11, DT, D], F32R)
        uo = sb("uo", [P, DT, D])
        cols = sb("cols", [P, 6, DT])
        rows = sb("rows", [P, 3, D])
        xn = sb("xn", [P, TT, D])
        x1 = sb("x1", [P, TT, D])
        o_tok = sb("o_tok", [P, TT, D])
        f_hi = sb("f_hi", [P, DT, L], F32R)
        f_lo = sb("f_lo", [P, DT, L], F32R)
        cell = sb("cell", [P, DT, L])
        cell_hi = sb("cell_hi", [P, DT, HALF], F32R)
        cell_lo = sb("cell_lo", [P, DT, HALF], F32R)
        cell_sum = sb("cell_sum", [P, DT, HALF])
        gates = sb("gates", [P, GATE_RING, HALF])
        whole = sb("whole", [P, 2, HALF])
        rest = sb("rest", [P, HALF])
        parts = sb("parts", [P, 2, 3, HALF], BF16)
        attn = sb("attn", [P, 2, 2, D])
        pre = attn
        o_raw = sb("o_raw", [P, HALF])
        inv_sum = sb("inv_sum", [P, 4, 4])
        max_half = sb("max_half", [P, 2, 2 * TT * 2])
        neg_max = sb("neg_max", [P, TT, 2])
        max_rest = sb("max_rest", [P, TT, 2])
        max_parts = sb("max_parts", [P, TT, 2, 3], BF16)
        max_rows = sb("max_rows", [6, L], BF16)
        cs = sb("cs", [P, DT, BATCH])
        cs_tanh = sb("cs_tanh", [P, DT, BATCH])
        silu = sb("silu", [P, DT, BATCH])
        modT = sb("modT", [P, 4, DT, BATCH])
        mod_rows = sb("mod_rows", [P, 2, BATCH, D])
        ga_bo = sb("ga_bo", [P, BATCH, D])
        stats = sb("stats", [P, 2, TT, 6])
        mean_var = sb("mean_var", [P, 2, TT, 2])
        var_eps = sb("var_eps", [P, 2, TT])
        rstd = sb("rstd", [P, 2, TT])
        minus_half = sb("minus_half", [P, TT])
        ident = sb("ident", [P, P])
        ident_bf = sb("ident_bf", [P, P], BF16)
        wmod = probs.rearrange("p a h l -> p (a h l)")[:, 0:DT * 6 * D].rearrange("p (t n) -> p t n", t=DT)
        silu_wide = probs.rearrange("p a h l -> p (a h l)")[:, DT * 6 * D:].rearrange(
            "p (t b n) -> p t b n", t=DT, b=BATCH)
        raw = [(WQ, WO, gates.rearrange("p n l -> p (n l)")[:, 0:3 * DT * D]),
               (WO, WX, o_tok.rearrange("p n d -> p (n d)")),
               (WX, UC + 1, x1.rearrange("p n d -> p (n d)"))]
        pre_all = stack.rearrange("p s k h l -> p (s k h l)").bitcast(F32).rearrange(
            "p (t n d) -> p t n d", t=BATCH, d=D)
        x1_chunk = probs.rearrange("p a h l -> p a (h l)").rearrange("p a (t n d) -> p a t n d", t=BATCH, d=D)
        result = [buf.rearrange("p c e -> p (c e)")[:, 0:BATCH * 2 * D].rearrange("p (t n d) -> p t n d", t=BATCH, d=D)
                  for buf in (xn, v_next, o_tok, v_now)]

        scoresT = [pb(f"scoresT{i}", [P, HALF]) for i in range(BANKS)]
        scores = [pb(f"scores{i}", [P, HALF]) for i in range(BANKS)]
        acc = pb("acc", [P, HALF])
        aux = pb("aux", [P, HALF])
        turns = [aux] + scores + scoresT

        c_in = sem("c_in")
        mod_in = sem("mod_in")
        qkv_in = sem("qkv_in")
        rest_in = sem("rest_in")
        xn_in = sem("xn_in")
        res_in = sem("res_in")
        waited = sem("waited")
        zeros = sem("zeros")
        consts = sem("consts")
        filled_once = sem("filled_once")
        ones = sem("ones")
        silu_seq = sem("silu_seq")
        biases_ready = sem("biases_ready")
        bias_in = sem("bias_in")
        mod_seq = sem("mod_seq")
        cs_tanhed = sem("cs_tanhed")
        silu_ready = sem("silu_ready")
        gate_rows = sem("gate_rows")
        mod_ready = sem("mod_ready")
        scoresT_full = sem("scoresT_full")
        exp_done = sem("exp_done")
        pv_done = sem("pv_done")
        acc_used = sem("acc_used")
        scores_full = sem("scores_full")
        scores_used = sem("scores_used")
        max_seq = sem("max_seq")
        max_split = sem("max_split")
        max_loaded = sem("max_loaded")
        full = sem("full")
        act_read = sem("act_read")
        dve_read = sem("dve_read")
        sums_inverted = sem("sums_inverted")
        stack_in = [sem(f"stack_in{s}") for s in range(RING)]
        v_in = [sem(f"v_in{c}") for c in range(len(V_CHUNKS))]
        v_added = sem("v_added")
        stats_ready = [sem(f"stats_ready{n}") for n in range(2)]
        mean_ready = [sem(f"mean_ready{n}") for n in range(2)]
        var_ready = [sem(f"var_ready{n}") for n in range(2)]
        rstd_ready = [sem(f"rstd_ready{n}") for n in range(2)]
        ln_done = [sem(f"ln_done{n}") for n in range(2)]
        w_split = sem("w_split")
        rounded = sem("rounded")
        split_features = sem("split_features")
        cell_rounded = sem("cell_rounded")
        cell_split = sem("cell_split")
        split_seq = sem("split_seq")
        split_done = sem("split_done")
        parts_out = [sem(f"parts_out{n}") for n in range(2)]
        res_biased = sem("res_biased")
        x1_ready = sem("x1_ready")
        x1_out = sem("x1_out")
        pre_out = [sem(f"pre_out{n}") for n in range(2)]
        gate_seq = sem("gate_seq")
        gate_sum = sem("gate_sum")
        cell_ready = sem("cell_ready")
        pre_in = sem("pre_in")
        x1_in = [sem(f"x1_in{n}") for n in range(2)]
        last_tanh = sem("last_tanh")
        last_gated = sem("last_gated")
        result_ready = [sem(f"result_ready{n}") for n in range(2)]
        out_done = [sem(f"out_done{n}") for n in range(2)]

        def alone(eng):
            eng.sem_inc(waited, 1)

        block = ctx.enter_context(nc.Block())
        before, first, mid, last, after = phases()

        def q_of(slot, h):
            return stack[:, slot, 0, h, :]

        def k_of(slot, h):
            return stack[:, slot, 1, h, :]

        def v_heads(v, c, n, h0=0, nh=HEADS):
            return v[:, c:c + n, h0 * VW:(h0 + nh) * VW].rearrange("p c (h e) -> p c h e", e=VW)

        def bank(ph, name, k):
            if (name, k) in ph.beside:
                return scores[0]
            n = sum(ph.order[name, k])
            return turns[n % len(turns)] if ph.by_turns and name != "maxT" else aux

        def qk_before(ph, name):
            return 8 * (ph.b + 1) if name == "hT" else 8 * (ph.b + (2 if ph.qkv else 1 if not ph.by_turns else 0))

        def by_token(ap):
            return ap.rearrange("p (c e) -> p c e", c=2)

        def tokens(ap):
            return ap.rearrange("(n p) d -> p n d", p=P)

        @block.tensor
        def _(pe):
            mm = nc.tensor.matmul

            def max_scores(ph, i, h, kh):
                hp, kt = divmod(i, KT)
                slot = (hp + 2) % RING
                m = 4 * i + 2 * h + kh
                n = 4 * KT * (GROUPS * ph.b + 2) + m
                if (kt, h, kh) == (0, 0, 0):
                    pe.wait_ge(stack_in[slot], 16 * len(BLOCKS) * (2 * ph.b + (hp + 2) // RING + 1))
                wait_past(pe, scores_used, freed(m, n))
                mm(scores[m % BANKS][:, :], q_of(slot, h)[0:STACK, kt * P:(kt + 1) * P],
                   k_of(slot, h)[0:STACK, kh * HALF:(kh + 1) * HALF], start=True, stop=True).then_inc(scores_full, 1)

            def exponents(ph, i, h, qh):
                hp, kt = divmod(i, KT)
                slot = hp % RING
                m = 4 * i + 2 * h + qh
                if (kt, h, qh) == (0, 0, 0):
                    pe.wait_ge(max_loaded, 32 * (GROUPS * ph.b + hp + 1))
                wait_past(pe, exp_done, freed(m, 4 * STEPS * ph.b + m))
                mm(scoresT[m % BANKS][:, :], k_of(slot, h)[0:ROWS, kt * P:(kt + 1) * P],
                   q_of(slot, h)[0:ROWS, qh * HALF:(qh + 1) * HALF], start=True, stop=True).then_inc(scoresT_full, 1)

            def weigh_values(ph, i):
                step = STEPS * ph.b + i - 1
                hp, kt = divmod((i - 1) % STEPS, KT)
                pe.wait_ge(exp_done, 4 * step + 4)
                if kt == 0:
                    wait_past(pe, acc_used, GROUPS * ph.b + hp)
                    pe.wait_ge(v_in[chunk_of(hp)], 16 * (ph.b + 1))
                for h in range(2):
                    for qh in range(2):
                        j = 32 * (2 * h + qh)
                        head = 2 * hp + h
                        one = mm(acc[j:j + 32, :], v_now[:, kt, head * VW:head * VW + 32],
                                 probs[:, (i - 1) % 2, h, qh * HALF:(qh + 1) * HALF],
                                 start=(kt == 0), stop=(kt == KT - 1))
                one.then_inc(pv_done, 1)


            def project_features(dst, et, operands):
                for hi, lo, u in operands:
                    for dt in range(DT):
                        w1, w2 = w_hi[:, u, dt, et * P:(et + 1) * P], w_lo[:, u, dt, et * P:(et + 1) * P]
                        begin, end = (u, dt) == (operands[0][2], 0), (u, dt) == (operands[-1][2], DT - 1)
                        mm(dst, w1, hi[:, dt, :], start=begin, stop=False)
                        mm(dst, w1, lo[:, dt, :], start=False, stop=False)
                        one = mm(dst, w2, hi[:, dt, :], start=False, stop=end)
                return one

            def project_tokens(dst, u, k):
                for c in range(2):
                    for dt in range(DT):
                        t = slice((2 * k + c) * P, (2 * k + c + 1) * P)
                        mm(by_token(dst)[:, c, :], f_hi[:, dt, t], w_hi[:, u, dt, :], start=(dt == 0), stop=False)
                        mm(by_token(dst)[:, c, :], f_hi[:, dt, t], w_lo[:, u, dt, :], start=False, stop=False)
                        one = mm(by_token(dst)[:, c, :], f_lo[:, dt, t], w_hi[:, u, dt, :], start=False,
                                 stop=(dt == DT - 1))
                return one

            def transpose_tokens(dst, src, k):
                th, dt = divmod(k, 2)
                for c in range(4):
                    one = nc.tensor.transpose(dst[:, c * P:(c + 1) * P], src[:, 4 * th + c, dt * P:(dt + 1) * P],
                                              ident[:, :])
                return one

            def wait_read(ph, name, k):
                pe.wait_ge(act_read if name in BY_ACT else dve_read, ph.read(name, k))

            def fill(ph, name, k):
                n = [(a, c) for _, a, c in ph.plan].index((name, k))
                by_turns = ph.by_turns
                back = len(turns) if by_turns and name != "maxT" else 1
                if (name, k) in ph.late[1:]:
                    back = 2
                if (name, k) in ph.beside[:1]:
                    pe.wait_ge(scores_used, 4 * STEPS * BATCH)
                elif n >= back:
                    wait_read(ph, *ph.plan[n - back][1:])
                elif n == 0:
                    wait_past(pe, act_read, ph.base[1])
                    wait_past(pe, dve_read, ph.base[0])
                dst = bank(ph, name, k)
                if name == "norm":
                    pe.wait_ge(acc_used, GROUPS * ph.b + k)
                    for c in range(4):
                        one = nc.tensor.transpose(dst[:, c * P:(c + 1) * P], o_raw[:, c * P:(c + 1) * P], ident[:, :])
                elif name == "maxT":
                    pe.wait_ge(max_split, GROUPS * ph.b + k + 2)
                    for qt in range(TT):
                        one = nc.tensor.transpose(dst.bitcast(BF16)[0:6, qt * P:(qt + 1) * P],
                                                  max_parts[:, qt, :, :].rearrange("p h a -> p (h a)"), ident_bf[:, :])
                elif name == "oT":
                    if by_turns:
                        wait_read(ph, "norm", 0)
                    one = transpose_tokens(dst, o_tok, k)
                elif name == "hT":
                    pe.wait_ge(ln_done[0], 2 * (ph.b + 1) + k // 2 + 1)
                    one = transpose_tokens(dst, xn, k)
                elif name == "h2T":
                    pe.wait_ge(ln_done[1], 2 * (ph.b - 1) + k // 2 + 1)
                    one = transpose_tokens(dst, xn, k)
                elif name == "qk":
                    th = k % 2
                    pe.wait_ge(split_features, ph.split("hT", 2 * th + 1))
                    half = slice(th * HALF, (th + 1) * HALF)
                    one = project_features(dst, k // 4, [(f_hi[:, :, half], f_lo[:, :, half], WQ + k // 2 % 2)])
                elif name == "v":
                    pe.wait_ge(split_features, ph.split("hT", 2 * (k // 2) + 1))
                    one = project_tokens(dst, WV, k)
                elif name == "wo":
                    pe.wait_ge(split_features, ph.split("oT", 2 * (k // 2) + 1))
                    one = project_tokens(dst, WO, k)
                elif name == "gate":
                    th, et, gate = k // 6, k // 3 % 2, k % 3
                    pe.wait_ge(split_features, ph.split("h2T", 2 * th + 1))
                    pe.wait_ge(cell_split, 2 * (ph.b - 1) + th + 1)
                    half = slice(th * HALF, (th + 1) * HALF)
                    one = project_features(dst, et, [(f_hi[:, :, half], f_lo[:, :, half], WF + gate),
                                                     (cell_hi, cell_lo, UF + gate)])
                elif name == "pre":
                    pe.wait_ge(split_features, ph.split("h2T", 2 * (k // 2) + 1))
                    one = project_tokens(dst, WX, k)
                elif name == "fin":
                    pe.wait_ge(cell_ready, 2 * BATCH + k // 2 + 1)
                    for c in range(2):
                        for dt in range(DT):
                            one = mm(by_token(dst)[:, c, :], cell[:, dt, (2 * k + c) * P:(2 * k + c + 1) * P],
                                     uo[:, dt, :], start=(dt == 0), stop=(dt == DT - 1))
                elif name == "modT":
                    for m in (2 * k, 2 * k + 1):
                        for dt in range(DT):
                            for kt in range(DT):
                                c0 = MOD_COLS[m] * D + dt * P
                                o = (m * DT + dt) * BATCH
                                one = mm(dst[:, o:o + BATCH], wmod[:, kt, c0:c0 + P], silu[:, kt, :],
                                         start=(kt == 0), stop=(kt == DT - 1))
                elif name == "mod_rows":
                    for c in range(2):
                        for kt in range(DT):
                            col = (GA, GB)[k // 2] * D
                            one = mm(by_token(dst)[:, c, :], silu_wide[:, kt, 2 * (k % 2) + c, :],
                                     wmod[:, kt, col:col + D], start=(kt == 0), stop=(kt == DT - 1))
                one.then_inc(full, 1)

            def steps(ph, prior):
                for i in range(STEPS):
                    ahead = maxima_run(ph, i)
                    for n in range(4):
                        if n == 3 and (prior or i):
                            weigh_values(ph, i)
                        if n == (3 if ahead else 2) and i in ph.at:
                            fill(ph, *ph.at[i])
                        exponents(ph, i, *divmod(n, 2))
                        if ahead:
                            max_scores(ph, i, *divmod(n, 2))

            pe.wait_ge(consts, 1)
            pe.wait_ge(silu_ready, 1)
            pe.wait_ge(mod_in, 16)
            for _, name, k in before.plan:
                if (name, k) == ("qk", 0):
                    pe.wait_ge(w_split, 2)
                if name == "maxT":
                    break
                fill(before, name, k)
            pe.wait_ge(act_read, before.read("mod_rows", 3))
            for i in range(STEPS - 2 * KT, STEPS):
                for h in range(2):
                    for kh in range(2):
                        max_scores(before, i, h, kh)
                if i == STEPS - KT + 1:
                    pe.wait_ge(act_read, before.end()[1] - 1)
                    pe.wait_ge(dve_read, before.end()[0])
                    fill(before, "maxT", GROUPS - 1)
            steps(first, False)
            pe.wait_ge(w_split, 6)
            pe.wait_ge(rest_in, 48)
            with pe.Fori(1, BATCH - 1) as b:
                steps(mid(b), True)
            steps(last, True)
            weigh_values(after, 0)
            pe.wait_ge(scores_used, 32 * GROUPS * BATCH)
            for _, name, k in after.plan:
                fill(after, name, k)

        @block.scalar
        def _(act):
            run = nc.scalar.activation

            def exponentials(ph, i):
                step = STEPS * ph.b + i
                wait_past(act, pv_done, step - 1)
                for h in range(2):
                    for qh in range(2):
                        m = 4 * i + 2 * h + qh
                        act.wait_ge(scoresT_full, 4 * STEPS * ph.b + m + 1)
                        run(probs[:, i % 2, h, qh * HALF:(qh + 1) * HALF], scoresT[m % BANKS],
                            ACT.Exp).then_inc(exp_done, 1)

            def evacuate_output(ph, k):
                act.wait_ge(pv_done, STEPS * ph.b + KT * k)
                nc.scalar.copy(o_raw[:, :], acc[:, :]).then_inc(acc_used, 1)

            def evacuate(ph, name, k):
                if name not in BY_ACT:
                    return
                act.wait_ge(full, ph.full(name, k))
                src = bank(ph, name, k)
                th, dt = divmod(k, 2)
                half = slice(th * HALF, (th + 1) * HALF)
                if name == "maxT":
                    wait_past(act, max_loaded, 32 * (GROUPS * ph.b + k + 1))
                    nc.scalar.copy(max_rows[:, :], src.bitcast(BF16)[0:6, :]).then_inc(act_read, 1)
                elif name in FEATURES:
                    at = ph.split(name, k)
                    if k >= 2 or name == "oT":
                        wait_past(act, split_features, at - 2)
                    else:
                        wait_past(act, split_done, qk_before(ph, name))
                    if name == "oT":
                        nc.scalar.copy(whole[:, k % 2, :], src).then_inc(act_read, 1)
                    else:
                        t, shift, scale = (ph.b + 1, SA, CA) if name == "hT" else (ph.b - 1, SB, CB)
                        alone(act)
                        run(whole[:, k % 2, :], src, ACT.Identity, bias=modT[:, shift, dt, bass.ds(t, 1)],
                            scale=modT[:, scale, dt, bass.ds(t, 1)]).then_inc(act_read, 1)
                elif name == "qk":
                    n, which, et = k, k // 2 % 2, k // 4
                    if n >= 2:
                        act.wait_ge(split_done, 8 * (ph.b + 1) + n - 1)
                    else:
                        act.wait_ge(split_features, ph.split("hT", n + 2))
                    run(whole[:, n % 2, :], src, ACT.Identity,
                        bias=cols[:, BQ + which, et:et + 1],
                        scale=1.0 if which else SCALE).then_inc(act_read, 1)
                elif name == "mod_rows":
                    b0 = 2 * (k % 2)
                    nc.scalar.copy(mod_rows[:, k // 2, b0:b0 + 2, :], by_token(src)).then_inc(act_read, 1)
                elif name == "gate":
                    et, gate = k // 3 % 2, k % 3
                    if k == 0:
                        act.wait_ge(cell_ready, 2 * ph.b)
                    elif k >= GATE_RING:
                        act.wait_ge(gate_sum, 4 * (ph.b - 1) + (k - GATE_RING) // 3 + 1)
                    run(gates[:, k % GATE_RING, :], src, ACT.Tanh, bias=cols[:, BF + gate, et:et + 1],
                        scale=1.0 if gate == 2 else 0.5).then_inc(act_read, 1)

            def steps(ph, prior):
                for i in range(STEPS):
                    exponentials(ph, i)
                    if i % KT == 0 and (prior or i):
                        evacuate_output(ph, i // KT)
                    if i in ph.at:
                        evacuate(ph, *ph.at[i])

            act.wait_ge(c_in, 16)
            run(cs_tanh[:, :, :], cs[:, :, :], ACT.Tanh, scale=0.5).then_inc(cs_tanhed, 1)
            act.wait_ge(mod_seq, 1)
            act.wait_ge(biases_ready, 1)
            for _, name, k in before.plan:
                evacuate(before, name, k)
                if (name, k) == ("qk", 3):
                    for n in range(2):
                        act.wait_ge(parts_out[n], 32)
                    part_of = pieces[0].rearrange("k c (g h d) t -> k c g h d t", g=GROUPS, h=2)
                    for block, qk, part in BLOCKS:
                        if qk == 0:
                            act.dma_start(stack[block * DK:(block + 1) * DK, 0, qk, :, :],
                                          part_of[qk, part, 0].rearrange("h d t -> d h t")).then_inc(stack_in[0], 16)
            steps(first, False)
            with act.Fori(1, BATCH - 1) as b:
                steps(mid(b), True)
            steps(last, True)
            evacuate_output(after, 0)
            for _, name, k in after.plan:
                evacuate(after, name, k)
                if name == "fin":
                    act.wait_ge(dve_read, after.read("fin", k))
                    r = result[k]
                    run(r[:, :, :, :], r[:, :, :, :], ACT.Tanh).then_inc(last_tanh, 1)

        @block.vector
        def _(dve):
            v = nc.vector

            def maximum(ph, i, h, kh):
                hp, kt = divmod(i, KT)
                m = 4 * i + 2 * h + kh
                dve.wait_ge(scores_full, 4 * KT * (GROUPS * ph.b + 2) + m + 1)
                col = (2 * kt + h) * 2 + kh
                v.tensor_reduce(max_half[:, hp % 2, col:col + 1], scores[m % BANKS][:, :], AX.X,
                                ALU.max).then_inc(scores_used, 1)

            def split_maxima(ph, hp, stage):
                g = GROUPS * ph.b + hp + 1
                if stage == 0:
                    dve.wait_ge(scores_used, 32 * (g + 1))
                    v.tensor_reduce(neg_max[:, :, :], max_half[:, (hp + 1) % 2, :].rearrange(
                        "p (q h k) -> p q h k", h=2, k=2), AX.X, ALU.max, negate=True).then_inc(max_seq, 1)
                elif stage == 1:
                    dve.wait_ge(max_seq, 4 * g + 1)
                    wait_past(dve, max_loaded, 32 * g)
                    v.tensor_copy(max_parts[:, :, :, 0], neg_max[:, :, :]).then_inc(max_seq, 1)
                    dve.wait_ge(max_seq, 4 * g + 2)
                    v.tensor_tensor(max_rest[:, :, :], neg_max[:, :, :], max_parts[:, :, :, 0],
                                    ALU.subtract).then_inc(max_seq, 1)
                else:
                    dve.wait_ge(max_seq, 4 * g + 3)
                    v.tensor_copy(max_parts[:, :, :, 1], max_rest[:, :, :]).then_inc(max_seq, 1)
                    dve.wait_ge(max_seq, 4 * g + 4)
                    v.tensor_tensor(max_parts[:, :, :, 2], max_rest[:, :, :], max_parts[:, :, :, 1],
                                    ALU.subtract).then_inc(max_split, 1)

            def norm_stats(which, src, tiles):
                for n in tiles:
                    one = v.bn_stats(stats[:, which, n, :], src[:, n, :])
                if tiles[-1] % 4 == 3:
                    one.then_inc(stats_ready[which], 1)

            def norm_moments(which, n, th):
                dve.wait_ge(stats_ready[which], 2 * n + th + 1)
                alone(dve)
                for t in range(4 * th, 4 * th + 4):
                    one = v.bn_aggr(mean_var[:, which, t, :], stats[:, which, t, :])
                one.then_inc(mean_ready[which], 1)
                dve.wait_ge(mean_ready[which], 2 * n + th + 1)
                v.tensor_scalar(var_eps[:, which, 4 * th:4 * th + 4], mean_var[:, which, 4 * th:4 * th + 4, 1], EPS,
                                None, ALU.add).then_inc(var_ready[which], 1)

            def norm_apply(which, n, src, tiles):
                dve.wait_ge(rstd_ready[which], 2 * n + tiles[0] // 4 + 1)
                for t in tiles:
                    one = v.tensor_scalar(xn[:, t, :], src[:, t, :], mean_var[:, which, t, 0:1],
                                          rstd[:, which, t:t + 1], ALU.subtract, ALU.mult)
                if tiles[-1] % 4 == 3:
                    one.then_inc(ln_done[which], 1)

            def split(ph, k):
                dve.wait_ge(act_read, ph.read("qk", k))
                wait_past(dve, parts_out[k % 2], 16 * (k // 2))
                src = whole[:, k % 2, :]
                part = [parts[:, k % 2, c, :] for c in range(3)]
                v.tensor_copy(part[0], src).then_inc(split_seq, 1)
                dve.wait_ge(split_seq, 3 * k + 1)
                v.tensor_tensor(rest[:, :], src, part[0], ALU.subtract).then_inc(split_seq, 1)
                dve.wait_ge(split_seq, 3 * k + 2)
                v.tensor_copy(part[1], rest[:, :]).then_inc(split_seq, 1)
                dve.wait_ge(split_seq, 3 * k + 3)
                v.tensor_tensor(part[2], rest[:, :], part[1], ALU.subtract).then_inc(split_done, 1)

            def split_half_tile(ph, name, k):
                th, dt = divmod(k, 2)
                half = slice(th * HALF, (th + 1) * HALF)
                dve.wait_ge(act_read, ph.read(name, k))
                v.tensor_copy(f_hi[:, dt, half], whole[:, k % 2, :]).then_inc(rounded, 1)
                dve.wait_ge(rounded, ph.split(name, k))
                v.tensor_tensor(f_lo[:, dt, half], whole[:, k % 2, :], f_hi[:, dt, half].bitcast(F32),
                                ALU.subtract).then_inc(split_features, 1)

            def gate_operands(n):
                return (gates[:, (GATES * n + m) % GATE_RING, :] for m in range(GATES))

            def keep_cell(ph, n):
                th, et = divmod(n, 2)
                f, _, _ = gate_operands(n)
                dve.wait_ge(act_read, ph.read("gate", 3 * n))
                dve.wait_ge(cell_ready, 2 * ph.b + th)
                v.scalar_tensor_tensor(f, f, 1.0, cell[:, et, th * HALF:(th + 1) * HALF], ALU.add,
                                       ALU.mult).then_inc(gate_seq, 1)

            def sum_gates(ph, n):
                th, et = divmod(n, 2)
                f, i, g = gate_operands(n)
                m = 4 * (ph.b - 1) + n
                dve.wait_ge(act_read, ph.read("gate", 3 * n + 2))
                dve.wait_ge(cell_ready, 2 * ph.b + th)
                v.scalar_tensor_tensor(i, i, 1.0, g, ALU.add, ALU.mult).then_inc(gate_seq, 1)
                dve.wait_ge(gate_seq, 2 * m + 2)
                v.tensor_tensor(cell_sum[:, et, :], f, i, ALU.add).then_inc(gate_sum, 1)

            def evacuate(ph, name, k):
                if name not in ("norm", "v", "wo", "pre"):
                    return
                dve.wait_ge(full, ph.full(name, k))
                src = bank(ph, name, k)
                if name == "norm":
                    hp = (k - 1) % GROUPS
                    o = src.rearrange("p (c j e) -> p c j e", c=4, j=4)
                    v.reciprocal(inv_sum[:, :, :], o[:, :, :, DK]).then_inc(sums_inverted, 1)
                    dve.wait_ge(sums_inverted, GROUPS * ph.b + k)
                    for h in range(2):
                        head = 2 * hp + h
                        one = v.tensor_tensor(
                            o_tok.rearrange("p (q c) d -> p q c d", q=2)[:, :, :, head * DK:(head + 1) * DK],
                            o.rearrange("p c j e -> p j c e")[:, 2 * h:2 * h + 2, :, 0:DK],
                            inv_sum.rearrange("p c j -> p j c")[:, 2 * h:2 * h + 2, :].unsqueeze(3).to_broadcast(
                                [P, 2, 4, DK]), ALU.mult)
                    one.then_inc(dve_read, 1)
                elif name == "v":
                    wait_past(dve, v_in[-1], 16 * (ph.b + 1))
                    bias = rows[:, BV, :].rearrange("p (h d) -> p h d", d=DK).unsqueeze(1).to_broadcast(
                        [P, 2, HEADS, DK])
                    one = v.tensor_tensor(v_heads(v_next, 2 * k, 2)[:, :, :, 0:DK],
                                          src.rearrange("p (c h d) -> p c h d", c=2, d=DK), bias, ALU.add)
                    if k == 0:
                        one.then_inc(v_added, 1)
                        dve.wait_ge(v_added, ph.b + 2)
                        first_key = v_heads(v_next, 0, 1)[0:1, 0, :, 0:DK]
                        one = v.tensor_scalar(first_key, first_key, 0.5, None, ALU.mult)
                    one.then_inc(dve_read, 1)
                elif name == "wo":
                    t = ph.b - 1
                    if k >= 2:
                        dve.wait_ge(x1_ready, 4 * t + k - 1)
                    if k == 0:
                        dve.wait_ge(res_biased, ph.b)
                    v.tensor_tensor(attn[:, k % 2, :, :], by_token(src), mod_rows[:, 0, bass.ds(t, 1), :].to_broadcast(
                        [P, 2, D]), ALU.mult).then_inc(dve_read, 1)
                elif name == "pre":
                    t = ph.b - 1
                    if k >= 2 and not ph.by_turns:
                        dve.wait_ge(pre_out[k % 2], 16 * (2 * t + 1))
                    dst = pre[:, k % 2, :, :] if not ph.by_turns else pre_all[:, t, 2 * k:2 * k + 2, :]
                    v.tensor_tensor(dst, by_token(src), rows[:, BH:BH + 1, :].to_broadcast(
                        [P, 2, D]), ALU.add).then_inc(dve_read, 1)

            def stats_after_attention(ph, k):
                dve.wait_ge(x1_ready, 4 * (ph.b - 1) + k + 1)
                norm_stats(1, x1, [2 * k, 2 * k + 1])

            def add_last(k):
                if k == 0:
                    dve.wait_ge(pre_in, 16 * (BATCH - 1))
                dve.wait_ge(dve_read, after.read("pre", k))
                dve.wait_ge(full, after.full("fin", k))
                v.tensor_tensor(result[k].rearrange("p t n d -> p t (n d)"),
                                bank(after, "fin", k).unsqueeze(1).to_broadcast([P, BATCH, HALF]),
                                pre_all[:, :, 2 * k:2 * k + 2, :].rearrange("p t n d -> p t (n d)"),
                                ALU.add).then_inc(dve_read, 1)

            def gate_last(k):
                dve.wait_ge(last_tanh, k + 1)
                r = result[k]
                gb = mod_rows[:, 1, :, :].unsqueeze(2).to_broadcast([P, BATCH, 2, D])
                v.tensor_tensor(r[:, :, :, :], r[:, :, :, :], gb, ALU.mult).then_inc(last_gated, 1)

            def add_residual_last(k):
                dve.wait_ge(last_gated, k + 1)
                dve.wait_ge(x1_in[k % 2], 16 * (BATCH - 1) * (k // 2 + 1))
                r = result[k]
                v.tensor_tensor(r[:, 0:2, :, :], r[:, 0:2, :, :], x1_chunk[:, k % 2, 0:2], ALU.add).then_inc(
                    result_ready[0], 1)

            def norm_after_attention(th):
                for k in (2 * th, 2 * th + 1):
                    stats_after_attention(after, k)
                norm_moments(1, BATCH - 1, th)
                norm_apply(1, BATCH - 1, x1, range(4 * th, 4 * th + 4))

            def steps(ph):
                for i in range(STEPS):
                    hp, kt = divmod(i, KT)
                    if kt < 3 and (ph.qkv or hp < GROUPS - 1):
                        split_maxima(ph, hp, kt)
                    if maxima_run(ph, i):
                        for h in range(2):
                            for kh in range(2):
                                maximum(ph, i, h, kh)
                    if i in ph.at:
                        evacuate(ph, *ph.at[i])
                    if ph.qkv and i == 4:
                        dve.wait_ge(xn_in, 16 * (ph.b + 2))
                    if ph.qkv and 4 <= i < 8:
                        norm_stats(0, xn, [2 * (i - 4), 2 * (i - 4) + 1])
                    if ph.qkv and i in (8, 9):
                        norm_moments(0, ph.b + 1, i - 8)
                    if ph.qkv and i in NORM1_APPLY:
                        norm_apply(0, ph.b + 1, xn, pair_of_tiles(i, NORM1_APPLY))
                    if ph.post and i in NORM2_STATS:
                        stats_after_attention(ph, NORM2_STATS.index(i))
                    if ph.post and i in NORM2_MOMENTS:
                        norm_moments(1, ph.b - 1, NORM2_MOMENTS.index(i))
                    if ph.post and i in NORM2_APPLY:
                        if ph.qkv:
                            dve.wait_ge(act_read, ph.read("hT", 3))
                        norm_apply(1, ph.b - 1, x1, pair_of_tiles(i, NORM2_APPLY))
                    name, k = ph.at.get(i - 1, (None, 0))
                    if name == "gate" and k % 3 == 0:
                        keep_cell(ph, k // 3)
                    if name == "gate" and k % 3 == 2:
                        sum_gates(ph, k // 3)

            dve.wait_ge(c_in, 16)
            dve.wait_ge(cs_tanhed, 1)
            v.scalar_tensor_tensor(silu[:, :, :], cs_tanh[:, :, :], 1.0, cs[:, :, :], ALU.add,
                                   ALU.mult).then_inc(silu_seq, 1)
            dve.wait_ge(silu_seq, 1)
            v.tensor_scalar(silu[:, :, :], silu[:, :, :], 0.5, None, ALU.mult).then_inc(silu_seq, 1)
            dve.wait_ge(silu_seq, 2)
            v.tensor_copy(silu_wide[:, :, :, :], silu[:, :, :].unsqueeze(3).to_broadcast(
                [P, DT, BATCH, P])).then_inc(silu_ready, 1)
            v.memset(v_next[:, :, :], 1.0)
            dve.wait_ge(xn_in, 16)
            for th in range(2):
                norm_stats(0, xn, list(range(4 * th, 4 * th + 4)))
                norm_moments(0, 0, th)
            for th in range(2):
                norm_apply(0, 0, xn, range(4 * th, 4 * th + 4))
            v.memset(v_now[:, :, :], 1.0).then_inc(filled_once, 1)
            dve.wait_ge(bias_in, 64)
            v.tensor_scalar(cols[:, BQ, :], cols[:, BQ, :], SCALE, None, ALU.mult)
            v.tensor_scalar(cols[:, BF:BI + 1, :], cols[:, BF:BI + 1, :], 0.5, None, ALU.mult).then_inc(biases_ready, 1)

            def evacuate_modulation(k):
                dve.wait_ge(full, before.full("modT", k))
                v.tensor_copy(modT[:, 2 * k:2 * k + 2, :, :].rearrange("p m t b -> p (m t b)"),
                              bank(before, "modT", k)[:, 2 * k * DT * BATCH:(2 * k + 2) * DT * BATCH]).then_inc(dve_read, 1)
                dve.wait_ge(dve_read, before.read("modT", k))
                v.tensor_scalar(modT[:, 2 * k + 1, :, :], modT[:, 2 * k + 1, :, :], 1.0, None, ALU.add).then_inc(mod_seq, 1)

            for _, name, k in before.plan:
                if name == "modT":
                    evacuate_modulation(k)
                if name == "hT":
                    split_half_tile(before, name, k)
                if name == "v":
                    evacuate(before, "v", k)
                if name == "qk" and k < 4:
                    split(before, k)
            for et in range(DT):
                v.tensor_copy(cell[:, et, :], cols[:, C0, et:et + 1].to_broadcast([P, L])).then_inc(cell_ready, 1)
            for i in range(STEPS - 2 * KT, STEPS):
                hp, kt = divmod(i, KT)
                if hp == GROUPS - 1 and kt == 0:
                    for stage in range(3):
                        split_maxima(before, hp, stage)
                for h in range(2):
                    for kh in range(2):
                        maximum(before, i, h, kh)
            dve.wait_ge(w_split, 4)
            steps(first)
            dve.wait_ge(mod_ready, 3)
            with dve.Fori(1, BATCH - 1) as b:
                steps(mid(b))
            steps(last)
            for _, name, k in after.plan:
                if name == "fin":
                    add_last(k)
                elif name in FEATURES:
                    split_half_tile(after, name, k)
                    if (name, k) == ("h2T", 1):
                        norm_after_attention(1)
                else:
                    evacuate(after, name, k)
                if (name, k) == ("wo", 1):
                    norm_after_attention(0)
                if name == "gate" and k % 3 == 0:
                    keep_cell(after, k // 3)
                if name == "gate" and k % 3 == 2:
                    sum_gates(after, k // 3)
                if (name, k) == ("fin", 1):
                    for chunk in range(2):
                        gate_last(chunk)
                if (name, k) == ("pre", 3):
                    for chunk in range(2):
                        add_residual_last(chunk)
            for chunk in range(2, 4):
                gate_last(chunk)
                add_residual_last(chunk)

        @block.gpsimd
        def _(pool):
            g = nc.gpsimd

            def split(ph, k):
                n, m = k, 8 * (ph.b + 1) + k
                pool.wait_ge(act_read, ph.read("qk", k))
                wait_past(pool, parts_out[n % 2], 16 * (4 * (ph.b + 1) + n // 2))
                alone(pool)
                src = whole[:, n % 2, :]
                part = [parts[:, n % 2, c, :] for c in range(3)]
                g.tensor_scalar(part[0], src, 1.0, 0.0, ALU.mult, ALU.add).then_inc(split_seq, 1)
                pool.wait_ge(split_seq, 3 * m + 1)
                g.tensor_tensor(rest[:, :], src, part[0], ALU.subtract).then_inc(split_seq, 1)
                pool.wait_ge(split_seq, 3 * m + 2)
                alone(pool)
                g.tensor_scalar(part[1], rest[:, :], 1.0, 0.0, ALU.mult, ALU.add).then_inc(split_seq, 1)
                pool.wait_ge(split_seq, 3 * m + 3)
                g.tensor_tensor(part[2], rest[:, :], part[1], ALU.subtract).then_inc(split_done, 1)

            def split_half_tile(ph, name, k):
                th, dt = divmod(k, 2)
                half = slice(th * HALF, (th + 1) * HALF)
                pool.wait_ge(act_read, ph.read(name, k))
                alone(pool)
                g.tensor_scalar(f_hi[:, dt, half], whole[:, k % 2, :], 1.0, 0.0, ALU.mult, ALU.add).then_inc(rounded, 1)
                pool.wait_ge(rounded, ph.split(name, k))
                g.tensor_tensor(f_lo[:, dt, half], whole[:, k % 2, :], f_hi[:, dt, half].bitcast(F32),
                                ALU.subtract).then_inc(split_features, 1)

            def split_weights(n):
                lo, hi, src = raw[n]
                u1, u2 = (u[:, lo:hi, :, :].rearrange("p u t d -> p (u t d)") for u in (w_hi, w_lo))
                g.tensor_scalar(u1, src, 1.0, 0.0, ALU.mult, ALU.add).then_inc(w_split, 1)
                pool.wait_ge(w_split, 2 * n + 1)
                g.tensor_tensor(u2, src, u1.bitcast(F32), ALU.subtract).then_inc(w_split, 1)

            def split_cell(t, th):
                half = slice(th * HALF, (th + 1) * HALF)
                g.tensor_scalar(cell_hi, cell[:, :, half], 1.0, 0.0, ALU.mult, ALU.add).then_inc(cell_rounded, 1)
                pool.wait_ge(cell_rounded, 2 * t + th + 1)
                g.tensor_tensor(cell_lo, cell[:, :, half], cell_hi.bitcast(F32), ALU.subtract).then_inc(cell_split, 1)

            def advance_cell(ph, th):
                if th == 0:
                    pool.wait_ge(full, ph.full("gate", 5))
                    alone(pool)
                    split_cell(ph.b - 1, 1)
                halve_cell(ph, th)
                if th == 1:
                    pool.wait_ge(full, ph.full("gate", 11))
                    alone(pool)
                    pool.wait_ge(cell_ready, 2 * ph.b + 1)
                    alone(pool)
                    split_cell(ph.b, 0)

            def inverse_deviation(which, n, th):
                pool.wait_ge(var_ready[which], 2 * n + th + 1)
                four = slice(4 * th, 4 * th + 4)
                g.tensor_tensor(rstd[:, which, four], var_eps[:, which, four], minus_half[:, four],
                                ALU.pow).then_inc(rstd_ready[which], 1)

            def bias_residual(ph):
                t = ph.b - 1
                pool.wait_ge(res_in, 16 * ph.b)
                g.tensor_tensor(x1[:, :, :], x1[:, :, :], ga_bo[:, bass.ds(t, 1), :].to_broadcast([P, TT, D]),
                                ALU.add).then_inc(res_biased, 1)

            def add_residual(ph, k):
                pool.wait_ge(dve_read, ph.read("wo", k))
                pool.wait_ge(res_biased, ph.b)
                two = x1[:, 2 * k:2 * k + 2, :]
                g.tensor_tensor(two, attn[:, k % 2, :, :], two, ALU.add).then_inc(x1_ready, 1)

            def add_residual_last(k):
                pool.wait_ge(last_gated, k + 1)
                pool.wait_ge(x1_in[k % 2], 16 * (BATCH - 1) * (k // 2 + 1))
                r, z = result[k], BATCH - 1
                g.tensor_tensor(r[:, 2:z, :, :], r[:, 2:z, :, :], x1_chunk[:, k % 2, 2:z], ALU.add)
                g.tensor_tensor(r[:, z, :, :], r[:, z, :, :], x1[:, 2 * k:2 * k + 2, :], ALU.add).then_inc(
                    result_ready[1], 1)

            def halve_cell(ph, th):
                pool.wait_ge(gate_sum, 4 * (ph.b - 1) + 2 * th + 2)
                alone(pool)
                g.tensor_scalar(cell[:, :, th * HALF:(th + 1) * HALF], cell_sum[:, :, :], 0.5, 0.0, ALU.mult,
                                ALU.add).then_inc(cell_ready, 1)

            def steps(ph):
                for i in range(STEPS):
                    name, k = ph.at.get(i, (None, 0))
                    if ph.post and i == 1:
                        bias_residual(ph)
                    if name == "qk":
                        split(ph, k)
                    if name in FEATURES:
                        split_half_tile(ph, name, k)
                    if name == "wo":
                        add_residual(ph, k)
                    if ph.qkv and i in (8, 9):
                        inverse_deviation(0, ph.b + 1, i - 8)
                    if ph.post and i in NORM2_MOMENTS:
                        inverse_deviation(1, ph.b - 1, NORM2_MOMENTS.index(i))
                    name, k = ph.at.get(i - 1, (None, 0))
                    if name == "gate" and k % 6 == 5:
                        advance_cell(ph, k // 6)

            g.memset(ident[:, :], 0.0)
            g.memset(ident_bf[:, :], 0.0)
            g.memset(minus_half[:, :], -0.5).then_inc(zeros, 1)
            pool.wait_ge(zeros, 1)
            g.affine_select(out=ident[:, :], in_=ident[:, :], compare_op=ALU.not_equal, fill=1.0, base=0,
                            pattern=[[-1, P]], channel_multiplier=1)
            g.affine_select(out=ident_bf[:, :], in_=ident_bf[:, :], compare_op=ALU.not_equal, fill=1.0, base=0,
                            pattern=[[-1, P]], channel_multiplier=1).then_inc(consts, 1)
            pool.wait_ge(consts, 1)
            g.memset(stack[STACK:ROWS, :, 1, :, :], 1.0).then_inc(ones, 1)
            pool.wait_ge(ones, 1)
            for th in range(2):
                inverse_deviation(0, 0, th)
            pool.wait_ge(qkv_in, 16)
            split_weights(0)
            pool.wait_ge(rest_in, 48)
            split_weights(1)
            split_weights(2)
            pool.wait_ge(split_done, 4)
            for k in range(4, 8):
                split(before, k)
            pool.wait_ge(cell_ready, 2)
            split_cell(0, 0)
            pool.wait_ge(bias_in, 64)
            pool.wait_ge(act_read, before.read("mod_rows", 3))
            for n in range(2):
                gate, sign, done = mod_rows[:, n], ga_bo, 4 * n
                g.tensor_scalar(sign, gate, 0.0, 2.0, ALU.is_ge, ALU.mult).then_inc(gate_rows, 1)
                pool.wait_ge(gate_rows, done + 1)
                g.tensor_scalar(sign, sign, 1.0, -1.0, ALU.mult, ALU.add).then_inc(gate_rows, 1)
                pool.wait_ge(gate_rows, done + 2)
                g.tensor_tensor(gate, gate, sign, ALU.mult).then_inc(gate_rows, 1)
                pool.wait_ge(gate_rows, done + 3)
                g.tensor_scalar(gate, gate, 0.25, 1.0, ALU.max, ALU.mult).then_inc(gate_rows, 1)
                pool.wait_ge(gate_rows, done + 4)
                g.tensor_tensor(gate, gate, sign, ALU.mult).then_inc(mod_ready, 1)
                pool.wait_ge(mod_ready, n + 1)
            g.tensor_tensor(ga_bo, mod_rows[:, 0, :, :], rows[:, BO:BO + 1, :].to_broadcast([P, BATCH, D]),
                            ALU.mult).then_inc(mod_ready, 1)
            pool.wait_ge(mod_ready, 3)
            steps(first)
            with pool.Fori(1, BATCH - 1) as b:
                steps(mid(b))
            steps(last)
            bias_residual(after)
            for _, name, k in after.plan:
                if name == "wo":
                    add_residual(after, k)
                if name == "wo" and k % 2:
                    inverse_deviation(1, BATCH - 1, k // 2)
                if (name, k) == ("gate", 5):
                    advance_cell(after, 0)
                if (name, k) == ("gate", 11):
                    add_residual_last(0)
                    halve_cell(after, 1)
            for chunk in range(1, 4):
                add_residual_last(chunk)

        @block.sync
        def _(sp):
            def load_stack(ph, hp):
                nb, h3 = (ph.b, hp + 3) if hp + 3 < GROUPS else (ph.b + 1, hp + 3 - GROUPS)
                slot = (hp + 3) % RING
                if h3 in (0, GROUPS // 2):
                    for n in range(2):
                        sp.wait_ge(parts_out[n], 64 * nb + (32 if h3 == 0 else 64))
                        alone(sp)
                wait_past(sp, scoresT_full, 4 * KT * (GROUPS * ph.b + hp))
                alone(sp)
                part_of = pieces[bass.ds(nb, 1)].rearrange("o k c (g h d) t -> (o k) c g h d t", g=GROUPS, h=2)
                for block, qk, part in BLOCKS:
                    if (ph.by_turns, h3, qk) == (True, 0, 0):
                        continue
                    r = block * DK
                    sp.dma_start(stack[r:r + DK, slot, qk, :, :], part_of[qk, part, h3].rearrange(
                        "h d t -> d h t")).then_inc(stack_in[slot], 16)

            def move_values(c, batch, groups_done):
                lo, hi = V_CHUNKS[c]
                wait_past(sp, pv_done, KT * groups_done)
                a, z = 2 * lo * VW, 2 * (hi + 1) * VW
                sp.dma_start(v_now[:, :, a:z], v_next[:, :, a:z]).then_inc(v_in[c], 16)

            def place_maxima(ph, hp):
                slot = (hp + 1) % RING
                sp.wait_ge(act_read, ph.read("maxT", hp))
                for h in range(2):
                    sp.dma_start(stack[STACK:ROWS, slot, 0, h, :], max_rows[3 * h:3 * h + 3, :]).then_inc(max_loaded, 16)

            def store_parts(ph, k):
                et, which, th = k // 4, k // 2 % 2, k % 2
                sp.wait_ge(split_done, 8 * (ph.b + 1) + k + 1)
                alone(sp)
                dst = pieces[bass.ds(ph.b + 1, 1), which, :, et * P:(et + 1) * P, th * HALF:(th + 1) * HALF]
                sp.dma_start(dst.rearrange("o c p t -> p (o c) t"), parts[:, k % 2, :, :]).then_inc(parts_out[k % 2], 16)

            def load_residual(ph):
                sp.wait_ge(act_read, ph.base[1])
                alone(sp)
                sp.dma_start(x1[:, :, :], tokens(x[bass.ds(ph.b - 1, 1)].rearrange("o n d -> (o n) d"))).then_inc(res_in, 16)

            def store_pre(ph, k):
                t = ph.b - 1
                sp.wait_ge(dve_read, ph.read("pre", k))
                alone(sp)
                sp.dma_start(pre_spill[:, bass.ds(t, 1), 2 * k:2 * k + 2, :].rearrange("p o n d -> p (o n) d"),
                             pre[:, k % 2, :, :]).then_inc(pre_out[k % 2], 16)

            def store_x1(ph):
                sp.wait_ge(x1_ready, 4 * ph.b)
                alone(sp)
                sp.dma_start(x1_spill[:, bass.ds(ph.b - 1, 1), :, :].rearrange("p o n d -> p (o n) d"),
                             x1[:, :, :]).then_inc(x1_out, 16)

            def store_result(k):
                for t in range(BATCH):
                    if t % 2 == 0:
                        sp.wait_ge(result_ready[t // 2], k + 1)
                    sp.dma_start(tokens(out[t])[:, 2 * k:2 * k + 2, :], result[k][:, t]).then_inc(out_done[k % 2], 16)

            def spilled(ph):
                sp.wait_ge(x1_out, 16 * ph.b)
                alone(sp)
                for n in range(2):
                    sp.wait_ge(pre_out[n], 32 * ph.b)
                    alone(sp)

            def steps(ph):
                for i in range(STEPS):
                    hp, kt = divmod(i, KT)
                    if kt == 4 and (ph.qkv or hp < GROUPS - 1):
                        place_maxima(ph, hp)
                    if i == 0 and ph.qkv:
                        sp.wait_ge(act_read, ph.base[1])
                        alone(sp)
                        sp.dma_start(xn[:, :, :], tokens(x[bass.ds(ph.b + 1, 1)].rearrange("o n d -> (o n) d"))
                                     ).then_inc(xn_in, 16)
                    if i == 0 and ph.post:
                        load_residual(ph)
                    if kt == 0 and (ph.qkv or hp + 3 < GROUPS):
                        load_stack(ph, hp)
                    if i == 1:
                        move_values(3, ph.b, GROUPS * ph.b)
                    if kt == 1 and hp >= 5 and ph.qkv:
                        move_values(hp - 5, ph.b + 1, GROUPS * ph.b + V_CHUNKS[hp - 5][1] + 1)
                    name, k = ph.at.get(i - 1, (None, 0))
                    if name == "qk":
                        store_parts(ph, k)
                    if name == "pre":
                        store_pre(ph, k)
                    if ph.post and i == 18:
                        store_x1(ph)
                    if ph.post and i == STEPS - 1:
                        spilled(ph)

            sp.dma_start(cs[:, :, :], cT.rearrange("(t p) b -> p t b", p=P)).then_inc(c_in, 16)
            sp.dma_start(xn[:, :, :], tokens(x[0])).then_inc(xn_in, 16)
            sp.dma_start(wmod, wmod_in.rearrange("(t p) n -> p t n", p=P)).then_inc(mod_in, 16)
            def load_weights(n):
                lo, hi, dst = raw[n]
                sp.dma_start(dst, w_all[:, lo:hi].rearrange("p u t d -> p (u t d)")).then_inc(rest_in if n else qkv_in, 16)

            load_weights(0)
            sp.dma_start(cols[:, :, :], cols_in).then_inc(bias_in, 16)
            for n in range(3):
                sp.dma_start(rows[:, n, :], rows_in[n].partition_broadcast(P)).then_inc(bias_in, 16)
            load_weights(1)
            load_weights(2)
            sp.dma_start(uo[:, :, :], w_all[:, UC + 1]).then_inc(rest_in, 16)
            sp.wait_ge(ones, 1)
            for k in range(4):
                store_parts(before, k)
            load_stack(before, 5)
            for k in range(4, 8):
                store_parts(before, k)
            load_stack(before, 6)
            sp.wait_ge(filled_once, 1)
            sp.wait_ge(dve_read, before.read("v", 3))
            for c in range(3):
                move_values(c, 0, 0)
            load_stack(before, 7)
            place_maxima(before, GROUPS - 1)
            steps(first)
            sp.wait_ge(w_split, 6)
            with sp.Fori(1, BATCH - 1) as b:
                steps(mid(b))
            steps(last)
            load_residual(after)
            sp.wait_ge(scoresT_full, 4 * STEPS * BATCH)
            for t in range(BATCH - 1):
                sp.dma_start(pre_all[:, t], pre_spill[:, t]).then_inc(pre_in, 16)

            def load_x1(k):
                for t in range(BATCH - 1):
                    sp.dma_start(x1_chunk[:, k % 2, t], x1_spill[:, t, 2 * k:2 * k + 2, :]).then_inc(x1_in[k % 2], 16)

            sp.wait_ge(pv_done, STEPS * BATCH)
            load_x1(0)
            load_x1(1)
            for k in range(4):
                store_result(k)
                if k < 2:
                    load_x1(k + 2)
            for n in range(2):
                sp.wait_ge(out_done[n], 16 * 2 * BATCH)

    return nc


def kernel(**inputs):
    import numpy as np
    import concourse.bacc as bacc
    from concourse.bass_utils import run_bass_kernel_spmd as run

    a = {name: np.asarray(v) for name, v in inputs.items()}
    matrices = [a[f"L0_attn_W{n}"] for n in "qkvo"] + [a[f"L0_ffn_{n}"] for n in
                                                      ("wf", "wi", "wc", "wo", "uf", "ui", "uc", "uo")]
    columns = [a["L0_attn_bq"], a["L0_attn_bk"], a["L0_ffn_bf"], a["L0_ffn_bi"], a["L0_ffn_bc"], a["L0_ffn_in_c"]]
    arrays = {
        "x": a["L0_attn_x"],
        "w_all": np.stack(matrices).transpose(2, 0, 1).reshape(DT, P, 12, D).transpose(1, 2, 0, 3),
        "cols": np.stack(columns).reshape(6, DT, P).transpose(2, 0, 1),
        "rows": np.stack([a["L0_attn_bv"], a["L0_attn_bo"], a["L0_ffn_bo"]]),
        "cT": a["L0_c"].T,
        "wmod": a["L0_wmod"],
    }
    arrays = {n: np.ascontiguousarray(v) for n, v in arrays.items()}
    nc = bacc.Bacc("TRN2", target_bir_lowering=False, num_devices=1,
                   dynamic_dma_scratch_size=4096)
    args = [nc.dram_tensor(f"in_{n}", v.shape, mybir.dt.from_np(v.dtype), kind="ExternalInput").ap() for n, v in arrays.items()]
    args += [nc.dram_tensor("pieces", (BATCH, 2, 3, D, L), BF16, kind="Internal").ap(),
             nc.dram_tensor("x1_spill", (P, BATCH, TT, D), F32, kind="Internal").ap(),
             nc.dram_tensor("pre_spill", (P, BATCH, TT, D), F32, kind="Internal").ap()]
    args.append(nc.dram_tensor("y", (BATCH, L, D), F32, kind="ExternalOutput").ap())
    adaln_layer(nc, *args)
    r = run(nc, [{f"in_{n}": v for n, v in arrays.items()}], core_ids=[0])
    return r.results[0]["y"]
```
